# Optimizing a Trainium2 kernel written in Bass

```python
import numpy as np
import jax
import jax.numpy as jnp

def _softmax(x, axis=-1):
    return jax.nn.softmax(x, axis=axis)

def _gelu(x):
    return jax.nn.gelu(x, approximate=True)

def _silu(x):
    return jax.nn.silu(x)

def _sigmoid(x):
    return jax.nn.sigmoid(x)

def _layernorm(x, axis=-1, eps=1e-05):
    m = jnp.mean(x, axis=axis, keepdims=True)
    v = jnp.var(x, axis=axis, keepdims=True)
    return (x - m) / jnp.sqrt(v + eps)

def _scatter_add(tgt, idx, src, axis=0):
    return tgt.at[idx].add(src)

def _segment_sum(src, seg, n):
    return jax.ops.segment_sum(src, seg, n)
kernel_name = 'mk_adj_preln_d2_adj_r2_2995f7'

def setup_inputs(seed: int=0):
    np.random.seed(seed)
    _w = jnp.asarray

    def _rec_inputs():
        import jax
        import jax.numpy as jnp
        _gk = jax.random.key(seed)
        x = -0.0005207 + 1.001 * jax.random.normal(jax.random.fold_in(_gk, 1), (16, 512, 128), jnp.float32)
        _a = jax.random.bernoulli(jax.random.fold_in(_gk, 2), 0.0078125, (16, 512, 512))
        _a = jnp.logical_or(_a, jnp.swapaxes(_a, -1, -2))
        _a = jnp.logical_or(_a, jnp.eye(512, dtype=bool))
        _af = _a.astype(jnp.float32)
        _af = _af * jax.random.uniform(jax.random.fold_in(_gk, 3), (16, 512, 512), jnp.float32, 0.05, 1)
        adj = _af
        _nm = jnp.ones((16, 512), dtype=bool)
        nodemask = jnp.where(_nm, 1.0, 0.0).astype(jnp.float32)
        return (x, adj, nodemask)
    x, adj, nodemask = _rec_inputs()

    def _L0_gnn_setup():
        import jax, jax.numpy as jnp
        import numpy as np
        B, N, F = (8, 512, 128)
        OUT, REL = (128, 16)
        NADJ = 7
        key = jax.random.key(seed)
        k0, k1, k2, k3, k4 = jax.random.split(key, 5)
        features = jax.random.normal(k0, (B, N, F), dtype=jnp.float32)
        A1 = jax.random.uniform(k1, (B, N, N), dtype=jnp.float32)
        A2 = jax.random.uniform(k2, (B, N, N), dtype=jnp.float32)
        W = jax.random.normal(k3, (NADJ, F + REL, OUT), dtype=jnp.float32) * 0.05
        W_edges = jnp.ones((NADJ, REL), dtype=jnp.float32)
        b = jax.random.uniform(k4, (N, OUT), dtype=jnp.float32, minval=-0.05, maxval=0.05)
        return {'features': features, 'A1': A1, 'A2': A2, 'W': W, 'W_edges': W_edges, 'b': b}
    _L0_gnn_all = _L0_gnn_setup()
    _L0_gnn_in = {k: v for k, v in _L0_gnn_all.items() if k in ('W', 'W_edges', 'b')}
    del _L0_gnn_all

    def _L1_gnn_setup():
        import jax, jax.numpy as jnp
        import numpy as np
        B, N, IN_DIM, OUT_DIM = (8, 1024, 128, 128)
        EDGE_P = 0.02
        MASK_P = 0.9
        key = jax.random.key(seed)
        ks = jax.random.split(key, 8)
        x = jax.random.normal(ks[0], (B, N, IN_DIM), dtype=jnp.float32)
        adj = (jax.random.uniform(ks[1], (B, N, N)) < EDGE_P).astype(jnp.float32)
        mask = (jax.random.uniform(ks[2], (B, N)) < MASK_P).astype(jnp.float32)
        lim1 = 1.0 / np.sqrt(IN_DIM)
        W = jax.random.uniform(ks[3], (OUT_DIM, IN_DIM), minval=-lim1, maxval=lim1, dtype=jnp.float32)
        b = jax.random.uniform(ks[4], (OUT_DIM,), minval=-lim1, maxval=lim1, dtype=jnp.float32)
        lim2 = 1.0 / np.sqrt(2 * OUT_DIM)
        a1 = jax.random.uniform(ks[5], (OUT_DIM,), minval=-lim2, maxval=lim2, dtype=jnp.float32)
        a2 = jax.random.uniform(ks[6], (OUT_DIM,), minval=-lim2, maxval=lim2, dtype=jnp.float32)
        att_b = jax.random.uniform(ks[7], (), minval=-lim2, maxval=lim2, dtype=jnp.float32)
        return {'x': x, 'adj': adj, 'mask': mask, 'W': W, 'b': b, 'a1': a1, 'a2': a2, 'att_b': att_b}
    _L1_gnn_all = _L1_gnn_setup()
    _L1_gnn_in = {k: v for k, v in _L1_gnn_all.items() if k in ('W', 'b', 'a1', 'a2', 'att_b')}
    del _L1_gnn_all
    return {'x': x, 'adj': adj, 'nodemask': nodemask, 'L0_gnn_W': _L0_gnn_in['W'], 'L0_gnn_W_edges': _L0_gnn_in['W_edges'], 'L0_gnn_b': _L0_gnn_in['b'], 'L1_gnn_W': _L1_gnn_in['W'], 'L1_gnn_b': _L1_gnn_in['b'], 'L1_gnn_a1': _L1_gnn_in['a1'], 'L1_gnn_a2': _L1_gnn_in['a2'], 'L1_gnn_att_b': _L1_gnn_in['att_b']}

def reference(x, adj, nodemask, L0_gnn_W, L0_gnn_W_edges, L0_gnn_b, L1_gnn_W, L1_gnn_b, L1_gnn_a1, L1_gnn_a2, L1_gnn_att_b):
    import jax
    import jax.numpy as jnp

    def _L0_gnn_ref(features, A1, A2, W, W_edges, b):
        import jax, jax.numpy as jnp
        import numpy as np
        B, N, F = (8, 512, 128)
        OUT, REL = (128, 16)
        NADJ = 7
        eye = jnp.zeros_like(A1) + jnp.eye(N, dtype=A1.dtype)
        shifted = jnp.roll(eye, 1, axis=0)
        A_fwd = [A1, A2, shifted]
        A_list = A_fwd + [jnp.swapaxes(a, 1, 2) for a in A_fwd]
        A_list.append(eye)
        A = jnp.stack(A_list, axis=0)
        HW = jnp.einsum('bnf,rfo->rbno', features, W[:, :F]) + jnp.einsum('rd,rdo->ro', W_edges, W[:, F:])[:, None, None, :]
        AHW = jnp.einsum('rbnm,rbmo->rbno', A, HW)
        out = jnp.max(AHW, axis=0) + b
        return out

    def _L1_gnn_ref(x, adj, mask, W, b, a1, a2, att_b):
        import jax, jax.numpy as jnp
        import numpy as np
        B, N, IN_DIM, OUT_DIM = (8, 1024, 128, 128)
        EDGE_P = 0.02
        MASK_P = 0.9
        h = jnp.einsum('bni,di->bnd', x, W) + b
        s1 = h @ a1
        s2 = h @ a2
        logits = s1[:, :, None] + s2[:, None, :] + att_b
        att = jax.nn.sigmoid(logits) * adj
        att = att * mask[:, :, None] * mask[:, None, :]
        att = att / (jnp.sum(att, axis=-1, keepdims=True) + 1e-08)
        h_new = jnp.einsum('bij,bjd->bid', att, h)
        return h_new * mask[:, :, None]
    h = jnp.maximum(_layernorm(x, axis=-1), 0.0)
    x = x + _L0_gnn_ref(h, adj, adj, L0_gnn_W, L0_gnn_W_edges, L0_gnn_b)
    h = jnp.maximum(_layernorm(x, axis=-1), 0.0)
    x = x + _L1_gnn_ref(h, adj, nodemask, L1_gnn_W, L1_gnn_b, L1_gnn_a1, L1_gnn_a2, L1_gnn_att_b)
    return x

_drawn_inputs = setup_inputs


def setup_inputs(seed=0):
    import zlib

    import numpy as np

    out = dict(_drawn_inputs(seed))
    spreads = {'L0_gnn_W_edges': (1.0, 0.2)}
    factors = {'L0_gnn_b': 4.515, 'L1_gnn_a1': 29.487, 'L1_gnn_a2': 36.645}
    for name, (base, spread) in spreads.items():
        noise = np.random.default_rng([zlib.crc32(name.encode()), seed]).standard_normal(out[name].shape)
        drawn = base * np.exp(spread * noise) if base else spread * noise
        out[name] = jnp.asarray(drawn.astype(out[name].dtype))
    for name, factor in factors.items():
        out[name] = (out[name] * factor).astype(out[name].dtype)
    return out
```

```python
from contextlib import ExitStack

import concourse.bass as bass
from concourse import mybir

F32 = mybir.dt.float32
F32R = mybir.dt.float32r
ALU = mybir.AluOpType
ACT = mybir.ActivationFunctionType
AX = mybir.AxisListType
P = 128
LN_EPS = 1e-5
DEN_EPS = 1e-8
SLOTS = (0, 1, 3, 4, 2, 5, 6)
SLOT_RUNS = ((0, 0, 2), (2, 3, 2), (4, 2, 1), (5, 5, 2))


def build(nc, x, adj, nodemask, w0, w_edges, b0, w1, b1, a1, a2, att_b, out):
    G, N, F = x.shape
    R, D = w_edges.shape
    C = N // P
    RO = R * F
    BANK = 512
    WIDE = F + 2
    assert F == P and R == 7 and C == 4 and N == BANK and G % 2 == 0 and R * D <= P

    x_d = x.rearrange("g (c p) f -> g p c f", p=P)
    adj_d = adj.rearrange("g (c p) n -> g p c n", p=P)
    out_d = out.rearrange("g (c p) f -> g p c f", p=P)

    with ExitStack() as ctx:
        def sb(name, shape, dt=F32):
            return ctx.enter_context(nc.sbuf_tensor(name, shape, dt))

        def ps(name, cols):
            return ctx.enter_context(nc.psum_tensor(name, [P, cols], F32))

        def sem(name):
            return ctx.enter_context(nc.semaphore(name))

        ident = sb("ident", [P, P])
        ones_r = sb("ones_r", [P, P], F32R)
        w0_full = sb("w0_full", [P, R, F])
        w0_hi = sb("w0_hi", [P, RO], F32R)
        w0_lo = sb("w0_lo", [P, RO], F32R)
        wrel = sb("wrel", [P, RO])
        edge_col = sb("edge_col", [P, 1])
        pick = sb("pick", [P, C * P])
        c4 = sb("c4", [P, C, RO], F32R)
        w1_nat = sb("w1_nat", [P, P])
        a_cols = sb("a_cols", [P, 2])
        b1_col = sb("b1_col", [P, 1])
        b1_wide = sb("b1_wide", [P, P])
        w1_full = sb("w1_full", [P, WIDE])
        w1_hi = sb("w1_hi", [P, WIDE], F32R)
        w1_lo = sb("w1_lo", [P, WIDE], F32R)
        wa_cols = sb("wa_cols", [P, 2])
        wa1_full = sb("wa1_full", [P, P])
        wa1_hi = sb("wa1_hi", [P, P], F32R)
        wa1_lo = sb("wa1_lo", [P, P], F32R)
        kappa = sb("kappa", [P, 1])
        bias_full = sb("bias_full", [P, WIDE])
        bias_r = sb("bias_r", [P, WIDE], F32R)
        b0_sb = sb("b0_sb", [P, C, F])
        mask_rows = sb("mask_rows", [G * C, P])
        mask_cols = sb("mask_cols", [P, G * C])
        ln_eps = sb("ln_eps", [P, C])
        minus_half = sb("minus_half", [P, C])
        minus_one = sb("minus_one", [P, C])

        x_sb = [sb(f"x_sb{i}", [P, C, F]) for i in range(2)]
        adj_sb = [sb(f"adj_sb{i}", [P, C, N]) for i in range(2)]
        adjT = [sb(f"adjT{i}", [P, C, N]) for i in range(2)]
        xb = [sb(f"xb{i}", [P, C, F]) for i in range(2)]
        x1 = [sb(f"x1_{i}", [P, C, F]) for i in range(2)]
        out_sb = [sb(f"out_sb{i}", [P, C, F]) for i in range(2)]
        h = [sb(f"h{i}", [P, C, F]) for i in range(2)]
        stats = sb("stats", [P, C, 6])
        moments1 = sb("moments1", [P, C, 2])
        moments2 = sb("moments2", [P, C, 2])
        ln1 = {n: sb(f"ln1_{n}", [P, C]) for n in ("var", "scale", "neg", "shift")}
        ln2 = {n: sb(f"ln2_{n}", [P, C]) for n in ("var", "scale", "neg", "shift")}
        hT_hi = sb("hT_hi", [P, N], F32R)
        hT_lo = sb("hT_lo", [P, N], F32R)
        atH_hi = sb("atH_hi", [P, N], F32R)
        atH_lo = sb("atH_lo", [P, N], F32R)
        aH_hi = sb("aH_hi", [P, N], F32R)
        aH_lo = sb("aH_lo", [P, N], F32R)
        adj_junk = sb("adj_junk", [P, C, N])
        sums = sb("sums", [P, 2 * C])
        sums_parts = sb("sums_parts", [P, P])
        sumsT = sb("sumsT", [P, P], F32R)
        mx = sb("mx", [P, C, F])
        pause = sb("pause", [P, 1])
        h2 = sb("h2", [P, C, F])
        h2T_hi = sb("h2T_hi", [P, N], F32R)
        h2T_lo = sb("h2T_lo", [P, N], F32R)
        m_cur = [sb(f"m_cur{i}", [P, C]) for i in range(2)]
        s2 = sb("s2", [P, C])
        hm = sb("hm", [P, C, WIDE])
        sig = sb("sig", [P, C, N])
        att = sb("att", [P, C, N])
        den = sb("den", [P, C])
        den_eps = sb("den_eps", [P, C])
        den_inv = sb("den_inv", [P, C])
        m_sq = sb("m_sq", [P, C])
        row_scale = sb("row_scale", [P, C])

        prod = [ps(f"prod{i}", 2 * BANK) for i in range(2)]
        turn = [ps(f"turn{i}", BANK) for i in range(2)]
        agg = ps("agg", BANK)
        s1_ps = ps("s1_ps", BANK)

        x_loaded = [sem(f"x_loaded{i}") for i in range(2)]
        adj_loaded = [sem(f"adj_loaded{i}") for i in range(2)]
        out_stored = [sem(f"out_stored{i}") for i in range(2)]
        ln1_stats_done = sem("ln1_stats_done")
        ln1_moments = sem("ln1_moments")
        ln1_pool = sem("ln1_pool")
        ln1_ready = sem("ln1_ready")
        h_ready = sem("h_ready")
        xb_ready = sem("xb_ready")
        hT_done = sem("hT_done")
        hT_hi_ready = sem("hT_hi_ready")
        hT_lo_ready = sem("hT_lo_ready")
        adjT_done = sem("adjT_done")
        adjT_ready = sem("adjT_ready")
        rowsums_ready = sem("rowsums_ready")
        atH_done = sem("atH_done")
        atH_hi_ready = sem("atH_hi_ready")
        atH_lo_ready = sem("atH_lo_ready")
        aH_done = sem("aH_done")
        aH_hi_ready = sem("aH_hi_ready")
        aH_lo_ready = sem("aH_lo_ready")
        sums_hi_done = sem("sums_hi_done")
        sums_ready = sem("sums_ready")
        sumsT_done = sem("sumsT_done")
        sumsT_ready = sem("sumsT_ready")
        prod_done = sem("prod_done")
        max_done = sem("max_done")
        x1_ready = sem("x1_ready")
        ln2_stats_done = sem("ln2_stats_done")
        ln2_moments = sem("ln2_moments")
        ln2_pool = sem("ln2_pool")
        ln2_ready = sem("ln2_ready")
        h2_ready = sem("h2_ready")
        h2T_done = sem("h2T_done")
        h2T_hi_ready = sem("h2T_hi_ready")
        h2T_lo_ready = sem("h2T_lo_ready")
        s1_done = sem("s1_done")
        hw_done = sem("hw_done")
        mask_ready = sem("mask_ready")
        s2_ready = sem("s2_ready")
        hm_ready = sem("hm_ready")
        sig_ready = sem("sig_ready")
        att_ready = sem("att_ready")
        att_done = sem("att_done")
        scale_steps = sem("scale_steps")
        out_ready = sem("out_ready")
        zeroed = sem("zeroed")
        ident_zero = sem("ident_zero")
        ident_ready = sem("ident_ready")
        w0_loaded = sem("w0_loaded")
        small_loaded = sem("small_loaded")
        sparse_loaded = sem("sparse_loaded")
        b0_loaded = sem("b0_loaded")
        setup_pe = sem("setup_pe")
        setup_dve = sem("setup_dve")
        w_ready = sem("w_ready")

        block = ctx.enter_context(nc.Block())

        def wait(eng, s, value):
            if not isinstance(value, int) or value > 0:
                eng.wait_ge(s, value)

        def loads(g, i):
            return 8 * (g - i) + 16

        SMALL = 9
        SPARSE = R + len(SLOT_RUNS)

        @block.sync
        def _(sp):
            def load_x(g, i):
                wait(sp, ln1_moments, g - 1)
                wait(sp, h_ready, g - 1)
                wait(sp, xb_ready, g - 1)
                sp.dma_start(x_sb[i][:, :, :], x_d[g]).then_inc(x_loaded[i], 16)

            def load_adj(g, i):
                turned = 4 * g - 4 if isinstance(g, int) else sp.snap(4 * g - 4)
                wait(sp, rowsums_ready, g - 1)
                wait(sp, adjT_done, turned)
                sp.dma_start(adj_sb[i][:, :, :], adj_d[g]).then_inc(adj_loaded[i], 16)

            def store(g, i):
                sp.wait_ge(out_ready, g + 1)
                sp.dma_start(out_d[g], out_sb[i][:, :, :]).then_inc(out_stored[i], 16)

            def step(g, b, lx=True, la=True):
                if lx:
                    load_x(g + 2, b)
                if la:
                    load_adj(g + 1, 1 - b)
                store(g - 1, 1 - b)

            sp.dma_start(x_sb[0][:, :, :], x_d[0]).then_inc(x_loaded[0], 16)
            sp.dma_start(adj_sb[0][:, :, :], adj_d[0]).then_inc(adj_loaded[0], 16)
            for s, r, n in SLOT_RUNS:
                sp.dma_start(w0_full[:, s:s + n, :],
                             w0[r:r + n, 0:F, :].rearrange("r f o -> f r o")).then_inc(w0_loaded, 16)
            sp.dma_start(x_sb[1][:, :, :], x_d[1]).then_inc(x_loaded[1], 16)
            sp.dma_start(adj_sb[1][:, :, :], adj_d[1]).then_inc(adj_loaded[1], 16)
            sp.dma_start(b0_sb[:, :, :], b0.rearrange("(c p) f -> p c f", p=P)).then_inc(b0_loaded, 16)
            load_x(2, 0)
            step(1, 1)
            with sp.Fori(0, (G - 4) // 2) as i:
                step(2 * i + 2, 0)
                step(2 * i + 3, 1)
            step(G - 2, 0, lx=False)
            step(G - 1, 1, lx=False, la=False)
            store(G - 1, 1)
            for i in range(2):
                sp.wait_ge(out_stored[i], 8 * G)

        @block.gpsimd
        def _(pool):
            def norm(t, moments, moments_ready, steps_done, ready, g):
                pool.wait_ge(moments_ready, g + 1)
                nc.gpsimd.tensor_tensor(t["var"][:, :], moments[:, :, 1], ln_eps[:, :],
                                        ALU.add).then_inc(steps_done, 1)
                nc.gpsimd.tensor_tensor(t["neg"][:, :], moments[:, :, 0], minus_one[:, :],
                                        ALU.mult).then_inc(steps_done, 1)
                pool.wait_ge(steps_done, 3 * g + 2)
                nc.gpsimd.tensor_tensor(t["scale"][:, :], t["var"][:, :], minus_half[:, :],
                                        ALU.pow).then_inc(steps_done, 1)
                pool.wait_ge(steps_done, 3 * g + 3)
                nc.gpsimd.tensor_tensor(t["shift"][:, :], t["neg"][:, :], t["scale"][:, :],
                                        ALU.mult).then_inc(ready, 1)

            def pre(g, i):
                wait(pool, h_ready, g)
                norm(ln1, moments1, ln1_moments, ln1_pool, ln1_ready, g)
                wait(pool, x1_ready, 4 * g - 4)
                pool.wait_ge(x_loaded[i], loads(g, i))
                nc.gpsimd.tensor_tensor(xb[i][:, :, :], x_sb[i][:, :, :], b0_sb[:, :, :],
                                        ALU.add).then_inc(xb_ready, 1)

            def step(g, b, has_pre=True):
                if has_pre:
                    pre(g + 1, 1 - b)
                wait(pool, h2_ready, g)
                norm(ln2, moments2, ln2_moments, ln2_pool, ln2_ready, g)

            nc.gpsimd.memset(ident[:, :], 0.0).then_inc(ident_zero, 1)
            nc.gpsimd.memset(wrel[:, :], 0.0)
            nc.gpsimd.memset(bias_full[:, :], 0.0)
            nc.gpsimd.memset(edge_col[:, :], 0.0).then_inc(zeroed, 1)
            pool.wait_ge(ident_zero, 1)
            nc.gpsimd.affine_select(out=ident[:, :], in_=ident[:, :], compare_op=ALU.not_equal, fill=1.0, base=0,
                                    pattern=[[-1, P]], channel_multiplier=1).then_inc(ident_ready, 1)
            nc.gpsimd.memset(ln_eps[:, :], LN_EPS)
            nc.gpsimd.memset(minus_half[:, :], -0.5)
            nc.gpsimd.memset(minus_one[:, :], -1.0).then_inc(ident_zero, 1)
            pool.wait_ge(ident_zero, 2)
            pool.wait_ge(b0_loaded, 16)
            pre(0, 0)
            step(0, 0)
            step(1, 1)
            step(2, 0)
            with pool.Fori(0, (G - 4) // 2) as i:
                step(2 * i + 3, 1)
                step(2 * i + 4, 0)
            step(G - 1, 1, has_pre=False)

        @block.scalar
        def _(act):
            def apply_norm(t, src, dst, done):
                for k in range(C):
                    last = nc.scalar.activation(dst[:, k, :], src[:, k, :], ACT.Relu,
                                                bias=t["shift"][:, k:k + 1], scale=t["scale"][:, k:k + 1])
                last.then_inc(done, 1)

            def row_sums(i, k):
                return nc.scalar.activation(adj_junk[:, k, :], adj_sb[i][:, k, :], ACT.Copy, accum_out=sums[:, k:k + 1])

            def pre(g, i):
                act.wait_ge(ln1_ready, g + 1)
                wait(act, aH_done, g - 1)
                apply_norm(ln1, x_sb[i], h[i], h_ready)

            def step(g, b, has_pre=True, has_a=True, has_b=True):
                if has_a:
                    act.wait_ge(hT_done, g + 1)
                    nc.scalar.activation(hT_hi[:, :], turn[0][:, :], ACT.Copy).then_inc(hT_hi_ready, 1)
                if has_b:
                    act.wait_ge(h2T_done, g)
                    nc.scalar.activation(h2T_hi[:, :], turn[1][:, :], ACT.Copy).then_inc(h2T_hi_ready, 1)
                if has_a:
                    wait(act, sums_ready, g)
                    act.wait_ge(adj_loaded[b], loads(g, b))
                    row_sums(b, 0)
                    row_sums(b, 1)
                    wait(act, att_ready, 4 * g - 4)
                    for k in range(C):
                        act.wait_ge(adjT_done, 4 * g + k + 1)
                        nc.scalar.activation(adjT[b][:, k, :], turn[1 - k % 2][:, :], ACT.Copy,
                                             accum_out=sums[:, C + k:C + k + 1]).then_inc(adjT_ready, 1)
                    act.wait_ge(atH_done, g + 1)
                    nc.scalar.activation(atH_hi[:, :], agg[:, :], ACT.Copy).then_inc(atH_hi_ready, 1)
                    row_sums(b, 2)
                    row_sums(b, 3).then_inc(rowsums_ready, 1)
                if has_b:
                    act.wait_ge(s1_done, g)
                    act.wait_ge(s2_ready, g)
                    wait(act, att_ready, 4 * g - 4)
                    for j in range(C):
                        nc.scalar.activation(sig[:, j, :], s1_ps[:, :], ACT.Sigmoid,
                                             bias=s2[:, j:j + 1]).then_inc(sig_ready, 1)
                if has_a:
                    act.wait_ge(sumsT_done, g + 1)
                    nc.scalar.activation(sumsT[:, :], turn[1][:, 0:P], ACT.Copy).then_inc(sumsT_ready, 1)
                    act.wait_ge(aH_done, g + 1)
                    nc.scalar.activation(aH_hi[:, :], agg[:, :], ACT.Copy).then_inc(aH_hi_ready, 1)
                if has_pre:
                    pre(g + 1, 1 - b)
                if has_a:
                    act.wait_ge(ln2_ready, g + 1)
                    wait(act, h2T_done, g)
                    apply_norm(ln2, x1[b], h2, h2_ready)

            act.wait_ge(zeroed, 1)
            for s, r, n in SLOT_RUNS:
                act.dma_start(edge_col[s * D:(s + n) * D, 0:1],
                              w_edges[r:r + n, :].rearrange("r (d a) -> (r d) a", a=1)).then_inc(sparse_loaded, 16)
            for s, r in enumerate(SLOTS):
                act.dma_start(wrel[s * D:(s + 1) * D, s * F:(s + 1) * F], w0[r, F:F + D, :]).then_inc(sparse_loaded, 16)
            act.dma_start(w1_nat[:, :], w1).then_inc(small_loaded, 16)
            act.dma_start(a_cols[:, 0:1], a1.rearrange("(p a) -> p a", a=1)).then_inc(small_loaded, 16)
            act.dma_start(a_cols[:, 1:2], a2.rearrange("(p a) -> p a", a=1)).then_inc(small_loaded, 16)
            act.dma_start(b1_col[:, :], b1.rearrange("(p a) -> p a", a=1)).then_inc(small_loaded, 16)
            act.dma_start(mask_rows[:, :], nodemask.rearrange("g (c p) -> (g c) p", p=P)).then_inc(small_loaded, 16)
            for q in (0, 32):
                act.dma_start(bias_full[q:q + 1, 0:P], b1.rearrange("(a p) -> a p", a=1)).then_inc(small_loaded, 16)
                act.dma_start(bias_full[q:q + 1, P:P + 1], att_b).then_inc(small_loaded, 16)
            act.wait_ge(x_loaded[0], 16)
            pre(0, 0)
            step(0, 0, has_b=False)
            step(1, 1)
            step(2, 0)
            with act.Fori(0, (G - 4) // 2) as i:
                step(2 * i + 3, 1)
                step(2 * i + 4, 0)
            step(G - 1, 1, has_pre=False)
            step(G, 0, has_pre=False, has_a=False)

        @block.vector
        def _(dve):
            def lo_part(dst, src, hi, ready):
                nc.vector.tensor_tensor(dst, src, hi.bitcast(F32), ALU.subtract).then_inc(ready, 1)

            def pre(g, i):
                dve.wait_ge(x_loaded[i], loads(g, i))
                for k in range(C):
                    last = nc.vector.bn_stats(stats[:, k, :], x_sb[i][:, k, :])
                last.then_inc(ln1_stats_done, 1)
                dve.wait_ge(ln1_stats_done, g + 1)
                wait(dve, ln1_ready, g)
                nc.vector.memset(pause[:, :], 0.0)
                for k in range(C):
                    last = nc.vector.bn_aggr(moments1[:, k, :], stats[:, k, :])
                last.then_inc(ln1_moments, 1)

            def layer1_inputs(g, i):
                nc.vector.tensor_copy(m_cur[i][:, :], mask_cols[:, bass.ds(C * g, C)]).then_inc(mask_ready, 1)
                hw = prod[1][:, :].rearrange("p (j w) -> p j w", j=C)
                dve.wait_ge(hw_done, g + 1)
                wait(dve, sig_ready, 4 * g)
                nc.vector.tensor_copy(s2[:, :], hw[:, :, F]).then_inc(s2_ready, 1)
                dve.wait_ge(mask_ready, g + 1)
                nc.vector.tensor_copy(hm[:, :, F], m_cur[i][:, :])
                nc.vector.tensor_tensor(hm[:, :, 0:F], hw[:, :, 0:F],
                                        m_cur[i][:, :].unsqueeze(2).to_broadcast([P, C, F]),
                                        ALU.mult).then_inc(hm_ready, 1)

            def finish(g, i):
                res = prod[0][:, :].rearrange("p (j w) -> p j w", j=C)
                dve.wait_ge(att_done, 4 * g + 4)
                nc.vector.tensor_tensor(den[:, :], res[:, :, F], m_cur[i][:, :], ALU.mult).then_inc(scale_steps, 1)
                nc.vector.tensor_tensor(m_sq[:, :], m_cur[i][:, :], m_cur[i][:, :], ALU.mult)
                dve.wait_ge(scale_steps, 4 * g + 1)
                nc.vector.tensor_scalar(den_eps[:, :], den[:, :], DEN_EPS, None, ALU.add).then_inc(scale_steps, 1)
                dve.wait_ge(scale_steps, 4 * g + 2)
                nc.vector.reciprocal(den_inv[:, :], den_eps[:, :]).then_inc(scale_steps, 1)
                dve.wait_ge(scale_steps, 4 * g + 3)
                nc.vector.tensor_tensor(row_scale[:, :], den_inv[:, :], m_sq[:, :], ALU.mult).then_inc(scale_steps, 1)
                dve.wait_ge(scale_steps, 4 * g + 4)
                wait(dve, out_stored[i], 8 * (g - i))
                for k in range(C):
                    last = nc.vector.scalar_tensor_tensor(out_sb[i][:, k, :], res[:, k, 0:F], row_scale[:, k:k + 1],
                                                          x1[i][:, k, :], ALU.mult, ALU.add)
                last.then_inc(out_ready, 1)

            def step(g, b, has_pre=True, has_a=True, has_b=True):
                if has_a:
                    dve.wait_ge(hT_hi_ready, g + 1)
                    lo_part(hT_lo[:, :], turn[0][:, :], hT_hi[:, :], hT_lo_ready)
                if has_b:
                    dve.wait_ge(h2T_hi_ready, g)
                    lo_part(h2T_lo[:, :], turn[1][:, :], h2T_hi[:, :], h2T_lo_ready)
                if has_pre:
                    pre(g + 1, 1 - b)
                if has_a:
                    dve.wait_ge(atH_hi_ready, g + 1)
                    lo_part(atH_lo[:, :], agg[:, :], atH_hi[:, :], atH_lo_ready)
                if has_b:
                    layer1_inputs(g - 1, 1 - b)
                if has_a:
                    dve.wait_ge(rowsums_ready, g + 1)
                    dve.wait_ge(adjT_ready, 4 * g + 4)
                    wait(dve, sumsT_done, g)
                    nc.vector.tensor_copy(sums_parts[:, 0:2 * C].bitcast(F32R), sums[:, :])
                    nc.vector.tensor_copy(sums_parts[:, 32:32 + 2 * C].bitcast(F32R), sums[:, :])\
                        .then_inc(sums_hi_done, 1)
                    dve.wait_ge(sums_hi_done, g + 1)
                    nc.vector.tensor_tensor(sums_parts[:, 2 * C:4 * C].bitcast(F32R), sums[:, :],
                                            sums_parts[:, 0:2 * C], ALU.subtract).then_inc(sums_ready, 1)
                if has_b:
                    wait(dve, att_done, 4 * g - 4)
                    for j in range(C):
                        dve.wait_ge(sig_ready, 4 * g - 4 + j + 1)
                        nc.vector.tensor_tensor(att[:, j, :], sig[:, j, :], adjT[1 - b][:, j, :],
                                                ALU.mult).then_inc(att_ready, 1)
                if has_a:
                    dve.wait_ge(aH_hi_ready, g + 1)
                    lo_part(aH_lo[:, :], agg[:, :], aH_hi[:, :], aH_lo_ready)
                    dve.wait_ge(xb_ready, g + 1)
                    wait(dve, ln2_ready, g)
                    wait(dve, h2_ready, g)
                    for k in range(C):
                        dve.wait_ge(prod_done, 4 * g + k + 1)
                        nc.vector.tensor_reduce(mx[:, k, :],
                                                prod[k % 2][:, 0:RO].rearrange("p (r o) -> p o r", r=R),
                                                AX.X, ALU.max).then_inc(max_done, 1)
                        dve.wait_ge(max_done, 4 * g + k + 1)
                        nc.vector.tensor_tensor(x1[b][:, k, :], mx[:, k, :], xb[b][:, k, :],
                                                ALU.add).then_inc(x1_ready, 1)
                        dve.wait_ge(x1_ready, 4 * g + k + 1)
                        nc.vector.bn_stats(stats[:, k, :], x1[b][:, k, :]).then_inc(ln2_stats_done, 1)
                    dve.wait_ge(ln2_stats_done, 4 * g + 4)
                    nc.vector.memset(pause[:, :], 0.0)
                    for k in range(C):
                        last = nc.vector.bn_aggr(moments2[:, k, :], stats[:, k, :])
                    last.then_inc(ln2_moments, 1)
                if has_b:
                    finish(g - 1, 1 - b)

            nc.vector.memset(ones_r[:, :].bitcast(F32), 1.0)
            nc.vector.memset(hm[:, :, F + 1:WIDE], 0.0)
            nc.vector.memset(w1_full[:, F + 1:WIDE], 0.0)
            nc.vector.memset(sums_parts[:, :], 0.0)
            nc.vector.memset(pick[:, :], 0.0).then_inc(setup_dve, 1)
            dve.wait_ge(setup_dve, 1)
            nc.vector.memset(sums_parts[:, 16:17], 1.0)
            nc.vector.memset(sums_parts[:, 48:49], 1.0)
            step_k = P + 1
            for q, shift in ((0, 0), (32, C)):
                for c in (0, 8, 32):
                    at = shift + c
                    nc.vector.memset(pick[q:q + 32, at:at + (C - 1) * step_k + 1:step_k], 1.0)
            for c in (16, 48):
                last = nc.vector.memset(pick[64:P, c:c + (C - 1) * P + 1:P], 1.0)
            last.then_inc(setup_dve, 1)
            pre(0, 0)
            dve.wait_ge(setup_dve, 2)
            dve.wait_ge(sparse_loaded, 16 * SPARSE)
            nc.vector.tensor_scalar(pick[:, :], pick[:, :], edge_col[:, 0:1], None, ALU.mult).then_inc(setup_dve, 1)
            dve.wait_ge(small_loaded, 16 * SMALL)
            nc.vector.tensor_copy(b1_wide[:, :], b1_col[:, 0:1].to_broadcast([P, P])).then_inc(setup_dve, 1)
            dve.wait_ge(w0_loaded, 16 * len(SLOT_RUNS))
            w0_flat = w0_full[:, :, :].rearrange("p r o -> p (r o)")
            nc.vector.tensor_copy(w0_hi[:, :], w0_flat).then_inc(setup_dve, 1)
            dve.wait_ge(setup_dve, 5)
            nc.vector.tensor_tensor(w0_lo[:, :], w0_flat, w0_hi[:, :].bitcast(F32), ALU.subtract)
            dve.wait_ge(setup_pe, 1)
            nc.vector.tensor_copy(w1_full[:, 0:F], turn[1][:, 0:P])
            nc.vector.tensor_copy(w1_full[:, F:F + 1], s1_ps[:, 1:2])
            nc.vector.tensor_copy(mask_cols[:, :], turn[1][:, P:P + G * C])
            nc.vector.tensor_copy(wa1_full[:, :], s1_ps[:, 0:1].to_broadcast([P, P]))
            nc.vector.reduce_sum(kappa[:, :], s1_ps[:, 2:4], AX.X).then_inc(setup_dve, 1)
            dve.wait_ge(setup_dve, 6)
            for q in (0, 32):
                last = nc.vector.tensor_tensor(bias_full[q:q + 1, F:F + 1], bias_full[q:q + 1, F:F + 1],
                                               kappa[q:q + 1, :], ALU.add)
            last.then_inc(setup_dve, 1)
            nc.vector.tensor_copy(w1_hi[:, :], w1_full[:, :])
            nc.vector.tensor_copy(wa1_hi[:, :], wa1_full[:, :])
            dve.wait_ge(setup_dve, 7)
            nc.vector.tensor_copy(bias_r[:, :], bias_full[:, :]).then_inc(setup_dve, 1)
            dve.wait_ge(setup_dve, 8)
            nc.vector.tensor_tensor(w1_lo[:, :], w1_full[:, :], w1_hi[:, :].bitcast(F32), ALU.subtract)
            nc.vector.tensor_tensor(wa1_lo[:, :], wa1_full[:, :], wa1_hi[:, :].bitcast(F32), ALU.subtract)
            nc.vector.tensor_tensor(bias_r[32:64, :], bias_full[32:64, :], bias_r[32:64, :].bitcast(F32),
                                    ALU.subtract)
            for k in range(C):
                dve.wait_ge(setup_pe, k + 2)
                nc.vector.tensor_copy(c4[:, k, :], prod[k % 2][:, 0:RO]).then_inc(setup_dve, 1)
                dve.wait_ge(setup_dve, 9 + 2 * k)
                nc.vector.tensor_tensor(c4[32:64, k, :], prod[k % 2][32:64, 0:RO],
                                        c4[32:64, k, :].bitcast(F32), ALU.subtract).then_inc(setup_dve, 1)
            dve.wait_ge(setup_dve, 8 + 2 * C)
            nc.vector.engine_nop().then_inc(w_ready, 1)
            step(0, 0, has_b=False)
            step(1, 1)
            step(2, 0)
            with dve.Fori(0, (G - 4) // 2) as i:
                step(2 * i + 3, 1)
                step(2 * i + 4, 0)
            step(G - 1, 1, has_pre=False)
            step(G, 0, has_pre=False, has_a=False)

        @block.tensor
        def _(pe):
            def mm(dst, lhsT, rhs, start, stop):
                return nc.tensor.matmul(dst, lhsT, rhs, start=start, stop=stop)

            def turn_rows(dst, src, done):
                for k in range(C):
                    last = nc.tensor.transpose(dst[:, k * P:(k + 1) * P], src[:, k, :], ident[:, :])
                last.then_inc(done, 1)

            def turn_adj(b, m):
                for c in range(C):
                    last = nc.tensor.transpose(turn[1 - m % 2][:, c * P:(c + 1) * P],
                                               adj_sb[b][:, c, m * P:(m + 1) * P], ident[:, :])
                last.then_inc(adjT_done, 1)

            def aggregate(b, rows, k):
                return mm(agg[:, :], h[b][:, k, :], rows[:, k, :], k == 0, k == C - 1)

            def step(g, b, has_a=True, has_b=True):
                if has_a:
                    pe.wait_ge(h_ready, g + 1)
                    wait(pe, adjT_ready, 4 * g)
                    turn_rows(turn[0], h[b], hT_done)
                if has_b:
                    pe.wait_ge(h2_ready, g)
                    pe.wait_ge(sumsT_ready, g)
                    turn_rows(turn[1], h2, h2T_done)
                if has_a:
                    pe.wait_ge(adj_loaded[b], loads(g, b))
                    wait(pe, aH_hi_ready, g)
                    wait(pe, aH_lo_ready, g)
                    aggregate(b, adj_sb[b], 0)
                    aggregate(b, adj_sb[b], 1)
                    wait(pe, h2T_hi_ready, g)
                    wait(pe, h2T_lo_ready, g)
                    turn_adj(b, 0)
                    pe.wait_ge(hT_hi_ready, g + 1)
                    pe.wait_ge(hT_lo_ready, g + 1)
                    turn_adj(b, 1)
                    aggregate(b, adj_sb[b], 2)
                    pe.wait_ge(adjT_ready, 4 * g + 1)
                    turn_adj(b, 2)
                    aggregate(b, adj_sb[b], 3).then_inc(atH_done, 1)
                    pe.wait_ge(adjT_ready, 4 * g + 2)
                    turn_adj(b, 3)
                if has_b:
                    pe.wait_ge(h2T_hi_ready, g)
                    pe.wait_ge(h2T_lo_ready, g)
                    wait(pe, sig_ready, 4 * g - 4)
                    mm(s1_ps[:, :], wa1_hi[:, :], h2T_hi[:, :], True, False)
                    mm(s1_ps[:, :], wa1_hi[:, :], h2T_lo[:, :], False, False)
                    mm(s1_ps[:, :], wa1_lo[:, :], h2T_hi[:, :], False, True).then_inc(s1_done, 1)
                    pe.wait_ge(max_done, 4 * g)
                    for j in range(C):
                        dst = prod[1][:, 256 * j:256 * j + WIDE]
                        nodes = slice(j * P, (j + 1) * P)
                        mm(dst, ones_r[:, :], bias_r[:, :], True, False)
                        mm(dst, h2T_hi[:, nodes], w1_hi[:, :], False, False)
                        mm(dst, h2T_hi[:, nodes], w1_lo[:, :], False, False)
                        last = mm(dst, h2T_lo[:, nodes], w1_hi[:, :], False, True)
                    last.then_inc(hw_done, 1)
                if has_a:
                    pe.wait_ge(adjT_ready, 4 * g + 4)
                    pe.wait_ge(atH_hi_ready, g + 1)
                    pe.wait_ge(atH_lo_ready, g + 1)
                    aggregate(b, adjT[b], 0)
                    aggregate(b, adjT[b], 1)
                    pe.wait_ge(sums_ready, g + 1)
                    nc.tensor.transpose(turn[1][:, 0:P], sums_parts[:, :], ident[:, :]).then_inc(sumsT_done, 1)
                    aggregate(b, adjT[b], 2)
                    aggregate(b, adjT[b], 3).then_inc(aH_done, 1)
                    pe.wait_ge(sumsT_ready, g + 1)
                    for k in range(C):
                        dst = prod[k % 2]
                        nodes = slice(k * P, (k + 1) * P)
                        if k == 0:
                            wait(pe, out_ready, g - 1)
                        elif k == 1 and has_b:
                            pe.wait_ge(hm_ready, g)
                        elif k >= 2:
                            pe.wait_ge(max_done, 4 * g + k - 1)
                        mm(dst[:, 0:BANK], sumsT[:, :], c4[:, k, 0:BANK], True, False)
                        mm(dst[:, BANK:RO], sumsT[:, :], c4[:, k, BANK:RO], True, False)
                        last = None
                        for hi, lo, c0, c1 in ((hT_hi, hT_lo, 4 * F, 7 * F), (atH_hi, atH_lo, 2 * F, 4 * F),
                                               (aH_hi, aH_lo, 0, 2 * F)):
                            if hi is aH_hi and k == 0:
                                pe.wait_ge(aH_hi_ready, g + 1)
                                pe.wait_ge(aH_lo_ready, g + 1)
                            end = hi is not atH_hi
                            mm(dst[:, c0:c1], hi[:, nodes], w0_hi[:, c0:c1], False, False)
                            mm(dst[:, c0:c1], hi[:, nodes], w0_lo[:, c0:c1], False, False)
                            last = mm(dst[:, c0:c1], lo[:, nodes], w0_hi[:, c0:c1], False, end)
                        last.then_inc(prod_done, 1)
                if has_b:
                    pe.wait_ge(hm_ready, g)
                    pe.wait_ge(att_ready, 4 * g)
                    if has_a:
                        pe.wait_ge(max_done, 4 * g + 3)
                    else:
                        pe.wait_ge(out_ready, g - 1)
                    for i in range(C):
                        for j in range(C):
                            last = mm(prod[0][:, 256 * i:256 * i + WIDE], att[:, j, i * P:(i + 1) * P],
                                      hm[:, j, :], j == 0, j == C - 1)
                        last.then_inc(att_done, 1)

            pe.wait_ge(ident_ready, 1)
            pe.wait_ge(small_loaded, 16 * SMALL)
            pe.wait_ge(setup_dve, 4)
            nc.tensor.transpose(turn[1][:, 0:P], w1_nat[:, :], ident[:, :])
            nc.tensor.transpose(turn[1][:, P:P + G * C], mask_rows[:, :], ident[0:G * C, 0:G * C])
            mm(s1_ps[:, 0:2], w1_nat[:, :], a_cols[:, :], True, True)
            mm(s1_ps[:, 2:4], b1_wide[:, :], a_cols[:, :], True, True).then_inc(setup_pe, 1)
            for k in range(C):
                if k >= 2:
                    pe.wait_ge(setup_dve, 8 + 2 * (k - 1))
                mm(prod[k % 2][:, 0:BANK], pick[:, k * P:(k + 1) * P], wrel[:, 0:BANK], True, True)
                mm(prod[k % 2][:, BANK:RO], pick[:, k * P:(k + 1) * P], wrel[:, BANK:RO], True, True)\
                    .then_inc(setup_pe, 1)
            pe.wait_ge(w_ready, 1)
            step(0, 0, has_b=False)
            step(1, 1)
            step(2, 0)
            with pe.Fori(0, (G - 4) // 2) as i:
                step(2 * i + 3, 1)
                step(2 * i + 4, 0)
            step(G - 1, 1)
            step(G, 0, has_a=False)


_INS = ['x', 'adj', 'nodemask', 'L0_gnn_W', 'L0_gnn_W_edges', 'L0_gnn_b', 'L1_gnn_W', 'L1_gnn_b', 'L1_gnn_a1',
        'L1_gnn_a2', 'L1_gnn_att_b']


def kernel(**inputs):
    import numpy as _np
    import concourse.bacc as _bacc
    from concourse import mybir as _mybir
    from concourse.bass_utils import run_bass_kernel_spmd as _run

    nc = _bacc.Bacc("TRN2", target_bir_lowering=False, num_devices=1)
    arrays, args = {}, []
    for name in _INS:
        a = _np.ascontiguousarray(inputs[name])
        if name == 'L1_gnn_att_b':
            a = a.reshape(1, 1)
        arrays[f"in_{name}_dram"] = a
        args.append(nc.dram_tensor(f"in_{name}_dram", a.shape, _mybir.dt.from_np(a.dtype), kind="ExternalInput").ap())
    shape = inputs['x'].shape
    args.append(nc.dram_tensor("out_0_dram", shape, _mybir.dt.float32, kind="ExternalOutput").ap())
    build(nc, *args)
    r = _run(nc, [arrays], core_ids=[0])
    return r.results[0]["out_0_dram"]
```

```python
from contextlib import ExitStack

import concourse.bass as bass
from concourse import mybir

F32 = mybir.dt.float32
F32R = mybir.dt.float32r
ALU = mybir.AluOpType
ACT = mybir.ActivationFunctionType
AX = mybir.AxisListType
P = 128
LN_EPS = 1e-5
DEN_EPS = 1e-8
SLOTS = (0, 1, 3, 4, 2, 5, 6)
SLOT_RUNS = ((0, 0, 2), (2, 3, 2), (4, 2, 1), (5, 5, 2))


def build(nc, x, adj, nodemask, w0, w_edges, b0, w1, b1, a1, a2, att_b, out):
    G, N, F = x.shape
    R, D = w_edges.shape
    C = N // P
    RO = R * F
    BANK = 512
    WIDE = F + 2
    assert F == P and R == 7 and C == 4 and N == BANK and G % 2 == 0 and R * D <= P

    x_d = x.rearrange("g (c p) f -> g p c f", p=P)
    adj_d = adj.rearrange("g (c p) n -> g p c n", p=P)
    out_d = out.rearrange("g (c p) f -> g p c f", p=P)

    with ExitStack() as ctx:
        def sb(name, shape, dt=F32):
            return ctx.enter_context(nc.sbuf_tensor(name, shape, dt))

        def ps(name, cols):
            return ctx.enter_context(nc.psum_tensor(name, [P, cols], F32))

        def sem(name):
            return ctx.enter_context(nc.semaphore(name))

        ident = sb("ident", [P, P])
        ones_r = sb("ones_r", [P, P], F32R)
        w0_full = sb("w0_full", [P, R, F])
        w0_hi = sb("w0_hi", [P, RO], F32R)
        w0_lo = sb("w0_lo", [P, RO], F32R)
        wrel = sb("wrel", [P, RO])
        edge_col = sb("edge_col", [P, 1])
        pick = sb("pick", [P, C * P])
        c4 = sb("c4", [P, C, RO], F32R)
        w1_nat = sb("w1_nat", [P, P])
        a_cols = sb("a_cols", [P, 2])
        b1_col = sb("b1_col", [P, 1])
        b1_wide = sb("b1_wide", [P, P])
        w1_full = sb("w1_full", [P, WIDE])
        w1_hi = sb("w1_hi", [P, WIDE], F32R)
        w1_lo = sb("w1_lo", [P, WIDE], F32R)
        wa_cols = sb("wa_cols", [P, 2])
        wa1_full = sb("wa1_full", [P, P])
        wa1_hi = sb("wa1_hi", [P, P], F32R)
        wa1_lo = sb("wa1_lo", [P, P], F32R)
        kappa = sb("kappa", [P, 1])
        bias_full = sb("bias_full", [P, WIDE])
        bias_r = sb("bias_r", [P, 2, WIDE], F32R)
        b0_sb = sb("b0_sb", [P, C, F])
        mask_rows = sb("mask_rows", [G * C, P])
        mask_cols = sb("mask_cols", [P, G * C])
        ln_eps = sb("ln_eps", [P, C])
        minus_half = sb("minus_half", [P, C])
        minus_one = sb("minus_one", [P, C])

        x_sb = [sb(f"x_sb{i}", [P, C, F]) for i in range(2)]
        adj_sb = [sb(f"adj_sb{i}", [P, C, N]) for i in range(2)]
        adjT = [sb(f"adjT{i}", [P, C, N]) for i in range(2)]
        xb = [sb(f"xb{i}", [P, C, F]) for i in range(2)]
        x1 = [sb(f"x1_{i}", [P, C, F]) for i in range(2)]
        out_sb = [sb(f"out_sb{i}", [P, C, F]) for i in range(2)]
        h = sb("h", [P, C, F])
        h_hi = sb("h_hi", [P, C, F], F32R)
        h_lo = sb("h_lo", [P, C, F], F32R)
        adj_hi = [sb(f"adj_hi{i}", [P, C, N], F32R) for i in range(2)]
        adj_lo = [sb(f"adj_lo{i}", [P, C, N], F32R) for i in range(2)]
        adjT_hi = sb("adjT_hi", [P, C, N], F32R)
        adjT_lo = sb("adjT_lo", [P, C, N], F32R)
        stats = sb("stats", [P, C, 6])
        stats2 = sb("stats2", [P, C, 6])
        moments1 = sb("moments1", [P, C, 2])
        moments2 = sb("moments2", [P, C, 2])
        ln1 = {n: sb(f"ln1_{n}", [P, C]) for n in ("var", "scale", "neg", "shift")}
        ln2 = {n: sb(f"ln2_{n}", [P, C]) for n in ("var", "scale", "neg", "shift")}
        hT_hi = sb("hT_hi", [P, N], F32R)
        hT_lo = sb("hT_lo", [P, N], F32R)
        atH_hi = sb("atH_hi", [P, N], F32R)
        atH_lo = sb("atH_lo", [P, N], F32R)
        aH_hi = sb("aH_hi", [P, N], F32R)
        aH_lo = sb("aH_lo", [P, N], F32R)
        sums = [sb(f"sums{i}", [P, 2 * C]) for i in range(2)]
        sums_parts = sb("sums_parts", [P, P])
        sumsT = sb("sumsT", [P, P], F32R)
        mx = sb("mx", [P, C, F])
        pause = sb("pause", [P, 2])
        h2 = sb("h2", [P, C, F])
        h2T_hi = sb("h2T_hi", [P, N], F32R)
        h2T_lo = sb("h2T_lo", [P, N], F32R)
        m_cur = [sb(f"m_cur{i}", [P, C]) for i in range(2)]
        s2 = sb("s2", [P, C])
        hm = sb("hm", [P, C, WIDE])
        sig = sb("sig", [P, C, N])
        att = sb("att", [P, C, N])
        den = sb("den", [P, C])
        den_eps = sb("den_eps", [P, C])
        den_inv = sb("den_inv", [P, C])
        m_sq = sb("m_sq", [P, C])
        row_scale = sb("row_scale", [P, C])

        prod = [ps(f"prod{i}", 2 * BANK) for i in range(2)]
        turn = [ps(f"turn{i}", BANK) for i in range(2)]
        agg_t = ps("agg_t", BANK)
        agg_a = ps("agg_a", BANK)

        x_loaded = [sem(f"x_loaded{i}") for i in range(2)]
        adj_loaded = [sem(f"adj_loaded{i}") for i in range(2)]
        out_free = [sem(f"out_free{i}") for i in range(2)]
        ln1_stats_done = sem("ln1_stats_done")
        ln1_moments = sem("ln1_moments")
        ln1_pool = sem("ln1_pool")
        ln1_ready = sem("ln1_ready")
        h_ready = sem("h_ready")
        xb_ready = sem("xb_ready")
        hT_done = sem("hT_done")
        hT_hi_ready = sem("hT_hi_ready")
        hT_lo_ready = sem("hT_lo_ready")
        adjT_done = sem("adjT_done")
        adjT_ready = sem("adjT_ready")
        adj_hi_ready = sem("adj_hi_ready")
        adj_lo_ready = sem("adj_lo_ready")
        adjT_hi_ready = sem("adjT_hi_ready")
        adjT_lo_ready = sem("adjT_lo_ready")
        h_hi_ready = sem("h_hi_ready")
        h_lo_ready = sem("h_lo_ready")
        atH_done = sem("atH_done")
        atH_hi_ready = sem("atH_hi_ready")
        atH_lo_ready = sem("atH_lo_ready")
        aH_done = sem("aH_done")
        aH_hi_ready = sem("aH_hi_ready")
        aH_lo_ready = sem("aH_lo_ready")
        sums_hi_done = sem("sums_hi_done")
        sums_ready = sem("sums_ready")
        sumsT_done = sem("sumsT_done")
        sumsT_ready = sem("sumsT_ready")
        prod_done = sem("prod_done")
        max_done = sem("max_done")
        x1_ready = sem("x1_ready")
        ln2_stats_done = sem("ln2_stats_done")
        ln2_moments = sem("ln2_moments")
        ln2_pool = sem("ln2_pool")
        ln2_ready = sem("ln2_ready")
        h2_ready = sem("h2_ready")
        h2T_done = sem("h2T_done")
        h2T_hi_ready = sem("h2T_hi_ready")
        h2T_lo_ready = sem("h2T_lo_ready")
        s1_done = sem("s1_done")
        hw_done = sem("hw_done")
        mask_ready = sem("mask_ready")
        s2_ready = sem("s2_ready")
        hm_ready = sem("hm_ready")
        sig_ready = sem("sig_ready")
        att_ready = sem("att_ready")
        att_done = sem("att_done")
        scale_steps = sem("scale_steps")
        out_ready = sem("out_ready")
        zeroed = sem("zeroed")
        ident_zero = sem("ident_zero")
        ident_ready = sem("ident_ready")
        w0_loaded = sem("w0_loaded")
        small_loaded = sem("small_loaded")
        sparse_loaded = sem("sparse_loaded")
        b0_loaded = sem("b0_loaded")
        setup_pe = sem("setup_pe")
        setup_dve = sem("setup_dve")
        w_ready = sem("w_ready")

        block = ctx.enter_context(nc.Block())

        def wait(eng, s, value):
            if not isinstance(value, int) or value > 0:
                eng.wait_ge(s, value)

        def loads(g, i):
            return 8 * (g - i) + 16

        def run(eng, step):
            def peeled(g):
                step(g, g % 2, has_pre=g < G - 1, has_a=g < G, has_b=1 <= g <= G, has_c=g >= 2)

            for g in range(3):
                peeled(g)
            with eng.Fori(0, (G - 4) // 2) as i:
                step(2 * i + 3, 1)
                step(2 * i + 4, 0)
            for g in range(G - 1, G + 2):
                peeled(g)

        SMALL = 9
        SPARSE = R + len(SLOT_RUNS)

        @block.sync
        def _(sp):
            def load_x(g, i):
                wait(sp, ln1_moments, g - 1)
                wait(sp, h_ready, g - 1)
                wait(sp, xb_ready, g - 1)
                sp.dma_start(x_sb[i][:, :, :], x_d[g]).then_inc(x_loaded[i], 16)

            def load_adj(g, i):
                used = 4 * g - 4 if isinstance(g, int) else sp.snap(4 * g - 4)
                wait(sp, adj_hi_ready, used)
                wait(sp, adj_lo_ready, used)
                wait(sp, adjT_done, used)
                sp.dma_start(adj_sb[i][:, :, :], adj_d[g]).then_inc(adj_loaded[i], 16)

            def store(g, i):
                sp.wait_ge(out_ready, g + 1)
                sp.dma_start(out_d[g], out_sb[i][:, :, :]).then_inc(out_free[i], 16)

            def step(g, b, load=True, done=True):
                if load:
                    load_x(g + 2, b)
                    load_adj(g + 2, b)
                if done:
                    store(g - 2, b)

            sp.dma_start(x_sb[0][:, :, :], x_d[0]).then_inc(x_loaded[0], 16)
            sp.dma_start(adj_sb[0][:, :, :], adj_d[0]).then_inc(adj_loaded[0], 16)
            for s, r, n in SLOT_RUNS:
                sp.dma_start(w0_full[:, s:s + n, :],
                             w0[r:r + n, 0:F, :].rearrange("r f o -> f r o")).then_inc(w0_loaded, 16)
            sp.dma_start(x_sb[1][:, :, :], x_d[1]).then_inc(x_loaded[1], 16)
            sp.dma_start(adj_sb[1][:, :, :], adj_d[1]).then_inc(adj_loaded[1], 16)
            sp.dma_start(b0_sb[:, :, :], b0.rearrange("(c p) f -> p c f", p=P)).then_inc(b0_loaded, 16)
            step(0, 0, done=False)
            step(1, 1, done=False)
            with sp.Fori(0, (G - 4) // 2) as i:
                step(2 * i + 2, 0)
                step(2 * i + 3, 1)
            for g in range(G - 2, G + 2):
                step(g, g % 2, load=False)
            for i in range(2):
                sp.wait_ge(out_free[i], 8 * G + 16)

        @block.gpsimd
        def _(pool):
            def norm(t, moments, moments_ready, steps_done, ready, g):
                pool.wait_ge(moments_ready, g + 1)
                nc.gpsimd.tensor_tensor(t["var"][:, :], moments[:, :, 1], ln_eps[:, :],
                                        ALU.add).then_inc(steps_done, 1)
                nc.gpsimd.tensor_tensor(t["neg"][:, :], moments[:, :, 0], minus_one[:, :],
                                        ALU.mult).then_inc(steps_done, 1)
                pool.wait_ge(steps_done, 3 * g + 2)
                nc.gpsimd.tensor_tensor(t["scale"][:, :], t["var"][:, :], minus_half[:, :],
                                        ALU.pow).then_inc(steps_done, 1)
                pool.wait_ge(steps_done, 3 * g + 3)
                nc.gpsimd.tensor_tensor(t["shift"][:, :], t["neg"][:, :], t["scale"][:, :],
                                        ALU.mult).then_inc(ready, 1)

            def pre(g, i):
                wait(pool, h_ready, g)
                norm(ln1, moments1, ln1_moments, ln1_pool, ln1_ready, g)
                wait(pool, x1_ready, 4 * g - 4)
                pool.wait_ge(x_loaded[i], loads(g, i))
                nc.gpsimd.tensor_tensor(xb[i][:, :, :], x_sb[i][:, :, :], b0_sb[:, :, :],
                                        ALU.add).then_inc(xb_ready, 1)

            def split_adj(g, i, ks):
                wait(pool, atH_done, g - 1)
                for k in ks:
                    pool.wait_ge(adj_hi_ready, 4 * g + k + 1)
                    nc.gpsimd.tensor_tensor(adj_lo[i][:, k, :], adj_sb[i][:, k, :], adj_hi[i][:, k, :].bitcast(F32),
                                            ALU.subtract).then_inc(adj_lo_ready, 1)

            def split_h(g):
                pool.wait_ge(h_hi_ready, g + 1)
                nc.gpsimd.tensor_tensor(h_lo[:, :, :], h[:, :, :], h_hi[:, :, :].bitcast(F32),
                                        ALU.subtract).then_inc(h_lo_ready, 1)

            def attention(g, i):
                wait(pool, att_done, 4 * g)
                for j in range(C):
                    pool.wait_ge(sig_ready, 4 * g + j + 1)
                    nc.gpsimd.tensor_tensor(att[:, j, :], sig[:, j, :], adjT[i][:, j, :],
                                            ALU.mult).then_inc(att_ready, 1)

            def step(g, b, has_pre=True, has_a=True, has_b=True, has_c=True):
                if has_b:
                    wait(pool, h2_ready, g - 1)
                    norm(ln2, moments2, ln2_moments, ln2_pool, ln2_ready, g - 1)
                if has_pre:
                    pre(g + 1, 1 - b)
                    split_adj(g + 1, 1 - b, (0, 1, 2, 3))
                    split_h(g + 1)
                if has_b:
                    attention(g - 1, 1 - b)

            nc.gpsimd.memset(ident[:, :], 0.0).then_inc(ident_zero, 1)
            nc.gpsimd.memset(wrel[:, :], 0.0)
            nc.gpsimd.memset(bias_full[:, :], 0.0)
            nc.gpsimd.memset(edge_col[:, :], 0.0).then_inc(zeroed, 1)
            pool.wait_ge(ident_zero, 1)
            nc.gpsimd.affine_select(out=ident[:, :], in_=ident[:, :], compare_op=ALU.not_equal, fill=1.0, base=0,
                                    pattern=[[-1, P]], channel_multiplier=1).then_inc(ident_ready, 1)
            nc.gpsimd.memset(ln_eps[:, :], LN_EPS)
            nc.gpsimd.memset(minus_half[:, :], -0.5)
            nc.gpsimd.memset(minus_one[:, :], -1.0).then_inc(ident_zero, 1)
            pool.wait_ge(ident_zero, 2)
            pool.wait_ge(b0_loaded, 16)
            pre(0, 0)
            split_adj(0, 0, (0, 1, 2, 3))
            split_h(0)
            run(pool, step)

        @block.scalar
        def _(act):
            def apply_norm(t, src, dst, done):
                for k in range(C):
                    last = nc.scalar.activation(dst[:, k, :], src[:, k, :], ACT.Relu,
                                                bias=t["shift"][:, k:k + 1], scale=t["scale"][:, k:k + 1])
                last.then_inc(done, 1)

            def split_adj(g, i, ks):
                act.wait_ge(adj_loaded[i], loads(g, i))
                wait(act, atH_done, g - 1)
                wait(act, sums_ready, g - 1)
                for k in ks:
                    nc.scalar.activation(adj_hi[i][:, k, :], adj_sb[i][:, k, :], ACT.Copy,
                                         accum_out=sums[i][:, k:k + 1]).then_inc(adj_hi_ready, 1)

            def take_adjT(g, b, m):
                act.wait_ge(adjT_done, 4 * g + m + 1)
                nc.scalar.activation(adjT[b][:, m, :], turn[1 - m % 2][:, :], ACT.Copy,
                                     accum_out=sums[b][:, C + m:C + m + 1]).then_inc(adjT_ready, 1)

            def hi_part(dst, src, ready):
                nc.scalar.activation(dst, src, ACT.Copy).then_inc(ready, 1)

            def split_h(g):
                act.wait_ge(h_ready, g + 1)
                wait(act, aH_done, g)
                hi_part(h_hi[:, :, :], h[:, :, :], h_hi_ready)

            def norm1(g, i):
                act.wait_ge(ln1_ready, g + 1)
                wait(act, hT_done, g)
                wait(act, h_lo_ready, g)
                apply_norm(ln1, x_sb[i], h, h_ready)

            def split_adjT(g, b, m):
                hi_part(adjT_hi[:, m, :], adjT[b][:, m, :], adjT_hi_ready)

            def norm2(g, i):
                act.wait_ge(ln2_ready, g + 1)
                wait(act, h2T_done, g)
                apply_norm(ln2, x1[i], h2, h2_ready)

            def step(g, b, has_pre=True, has_a=True, has_b=True, has_c=True):
                if has_a:
                    act.wait_ge(hT_done, g + 1)
                    hi_part(hT_hi[:, :], turn[0][:, :], hT_hi_ready)
                    wait(act, att_ready, 4 * g - 4)
                    take_adjT(g, b, 0)
                if has_pre:
                    split_adj(g + 1, 1 - b, (0,))
                if has_a:
                    take_adjT(g, b, 1)
                    wait(act, aH_done, g)
                    act.wait_ge(adjT_ready, 4 * g + 1)
                    split_adjT(g, b, 0)
                    take_adjT(g, b, 2)
                    act.wait_ge(adjT_ready, 4 * g + 2)
                    split_adjT(g, b, 1)
                    take_adjT(g, b, 3)
                if has_b:
                    norm2(g - 1, 1 - b)
                if has_a:
                    act.wait_ge(adjT_ready, 4 * g + 4)
                    split_adjT(g, b, 2)
                    split_adjT(g, b, 3)
                    act.wait_ge(atH_done, g + 1)
                    hi_part(atH_hi[:, :], agg_t[:, :], atH_hi_ready)
                if has_b:
                    act.wait_ge(h2T_done, g)
                    hi_part(h2T_hi[:, :], turn[1][:, :], h2T_hi_ready)
                if has_pre:
                    split_adj(g + 1, 1 - b, (1, 2, 3))
                if has_a:
                    act.wait_ge(aH_done, g + 1)
                    hi_part(aH_hi[:, :], agg_a[:, :], aH_hi_ready)
                    act.wait_ge(sumsT_done, g + 1)
                    hi_part(sumsT[:, :], turn[0][:, 0:P], sumsT_ready)
                if has_pre:
                    norm1(g + 1, 1 - b)
                    split_h(g + 1)
                if has_b:
                    act.wait_ge(s1_done, g)
                    act.wait_ge(s2_ready, g)
                    wait(act, att_ready, 4 * g - 4)
                    for j in range(C):
                        nc.scalar.activation(sig[:, j, :], agg_t[:, :], ACT.Sigmoid,
                                             bias=s2[:, j:j + 1]).then_inc(sig_ready, 1)

            act.wait_ge(zeroed, 1)
            for s, r, n in SLOT_RUNS:
                act.dma_start(edge_col[s * D:(s + n) * D, 0:1],
                              w_edges[r:r + n, :].rearrange("r (d a) -> (r d) a", a=1)).then_inc(sparse_loaded, 16)
            for s, r in enumerate(SLOTS):
                act.dma_start(wrel[s * D:(s + 1) * D, s * F:(s + 1) * F], w0[r, F:F + D, :]).then_inc(sparse_loaded, 16)
            act.dma_start(w1_nat[:, :], w1).then_inc(small_loaded, 16)
            act.dma_start(a_cols[:, 0:1], a1.rearrange("(p a) -> p a", a=1)).then_inc(small_loaded, 16)
            act.dma_start(a_cols[:, 1:2], a2.rearrange("(p a) -> p a", a=1)).then_inc(small_loaded, 16)
            act.dma_start(b1_col[:, :], b1.rearrange("(p a) -> p a", a=1)).then_inc(small_loaded, 16)
            act.dma_start(mask_rows[:, :], nodemask.rearrange("g (c p) -> (g c) p", p=P)).then_inc(small_loaded, 16)
            for q in (0, 32):
                act.dma_start(bias_full[q:q + 1, 0:P], b1.rearrange("(a p) -> a p", a=1)).then_inc(small_loaded, 16)
                act.dma_start(bias_full[q:q + 1, P:P + 1], att_b).then_inc(small_loaded, 16)
            act.wait_ge(x_loaded[0], 16)
            norm1(0, 0)
            split_h(0)
            split_adj(0, 0, (0, 1, 2, 3))
            run(act, step)

        @block.vector
        def _(dve):
            def lo_part(dst, src, hi, ready):
                nc.vector.tensor_tensor(dst, src, hi.bitcast(F32), ALU.subtract).then_inc(ready, 1)

            def pre(g, i):
                dve.wait_ge(x_loaded[i], loads(g, i))
                for k in range(C):
                    last = nc.vector.bn_stats(stats[:, k, :], x_sb[i][:, k, :])
                last.then_inc(ln1_stats_done, 1)
                dve.wait_ge(ln1_stats_done, g + 1)
                wait(dve, ln1_ready, g)
                nc.vector.memset(pause[:, 0:1], 0.0)
                for k in range(C):
                    last = nc.vector.bn_aggr(moments1[:, k, :], stats[:, k, :])
                last.then_inc(ln1_moments, 1)

            def layer1_inputs(g, i):
                nc.vector.tensor_copy(m_cur[i][:, :], mask_cols[:, bass.ds(C * g, C)]).then_inc(mask_ready, 1)
                hw = prod[1][:, :].rearrange("p (j w) -> p j w", j=C)
                dve.wait_ge(hw_done, g + 1)
                wait(dve, sig_ready, 4 * g)
                nc.vector.tensor_copy(s2[:, :], hw[:, :, F]).then_inc(s2_ready, 1)
                dve.wait_ge(mask_ready, g + 1)
                nc.vector.tensor_copy(hm[:, :, F], m_cur[i][:, :])
                nc.vector.tensor_tensor(hm[:, :, 0:F], hw[:, :, 0:F],
                                        m_cur[i][:, :].unsqueeze(2).to_broadcast([P, C, F]),
                                        ALU.mult).then_inc(hm_ready, 1)

            def finish(g, i):
                res = prod[0][:, :].rearrange("p (j w) -> p j w", j=C)
                dve.wait_ge(att_done, 4 * g + 4)
                nc.vector.tensor_tensor(den[:, :], res[:, :, F], m_cur[i][:, :], ALU.mult).then_inc(scale_steps, 1)
                nc.vector.tensor_tensor(m_sq[:, :], m_cur[i][:, :], m_cur[i][:, :], ALU.mult)
                dve.wait_ge(scale_steps, 4 * g + 1)
                nc.vector.tensor_scalar(den_eps[:, :], den[:, :], DEN_EPS, None, ALU.add).then_inc(scale_steps, 1)
                dve.wait_ge(scale_steps, 4 * g + 2)
                nc.vector.reciprocal(den_inv[:, :], den_eps[:, :]).then_inc(scale_steps, 1)
                dve.wait_ge(scale_steps, 4 * g + 3)
                nc.vector.tensor_tensor(row_scale[:, :], den_inv[:, :], m_sq[:, :], ALU.mult).then_inc(scale_steps, 1)
                dve.wait_ge(scale_steps, 4 * g + 4)
                dve.wait_ge(out_free[i], loads(g, i))
                for k in range(C):
                    last = nc.vector.scalar_tensor_tensor(out_sb[i][:, k, :], res[:, k, 0:F], row_scale[:, k:k + 1],
                                                          x1[i][:, k, :], ALU.mult, ALU.add)
                last.then_inc(out_ready, 1)

            def split_adjT(g, b, m):
                dve.wait_ge(adjT_hi_ready, 4 * g + m + 1)
                lo_part(adjT_lo[:, m, :], adjT[b][:, m, :], adjT_hi[:, m, :], adjT_lo_ready)

            def split_sums(g, b):
                dve.wait_ge(adj_hi_ready, 4 * g + 4)
                dve.wait_ge(adjT_ready, 4 * g + 4)
                wait(dve, sumsT_done, g)
                nc.vector.tensor_copy(sums_parts[:, 0:2 * C].bitcast(F32R), sums[b][:, :])
                nc.vector.tensor_copy(sums_parts[:, 32:32 + 2 * C].bitcast(F32R), sums[b][:, :])\
                    .then_inc(sums_hi_done, 1)
                dve.wait_ge(sums_hi_done, g + 1)
                nc.vector.tensor_tensor(sums_parts[:, 2 * C:4 * C].bitcast(F32R), sums[b][:, :],
                                        sums_parts[:, 0:2 * C], ALU.subtract).then_inc(sums_ready, 1)

            def x1_max(g, b, k):
                dve.wait_ge(prod_done, 4 * g + k + 1)
                nc.vector.tensor_reduce(mx[:, k, :], prod[k % 2][:, 0:RO].rearrange("p (r o) -> p o r", r=R),
                                        AX.X, ALU.max).then_inc(max_done, 1)
                if k > 0:
                    x1_stats(g, b, k - 1)
                dve.wait_ge(max_done, 4 * g + k + 1)
                nc.vector.tensor_tensor(x1[b][:, k, :], mx[:, k, :], xb[b][:, k, :], ALU.add).then_inc(x1_ready, 1)

            def x1_stats(g, b, k):
                dve.wait_ge(x1_ready, 4 * g + k + 1)
                nc.vector.bn_stats(stats2[:, k, :], x1[b][:, k, :]).then_inc(ln2_stats_done, 1)

            def step(g, b, has_pre=True, has_a=True, has_b=True, has_c=True):
                if has_a:
                    dve.wait_ge(hT_hi_ready, g + 1)
                    lo_part(hT_lo[:, :], turn[0][:, :], hT_hi[:, :], hT_lo_ready)
                if has_pre:
                    pre(g + 1, 1 - b)
                if has_a:
                    for m in range(C):
                        split_adjT(g, b, m)
                    dve.wait_ge(atH_hi_ready, g + 1)
                    lo_part(atH_lo[:, :], agg_t[:, :], atH_hi[:, :], atH_lo_ready)
                if has_b:
                    dve.wait_ge(h2T_hi_ready, g)
                    lo_part(h2T_lo[:, :], turn[1][:, :], h2T_hi[:, :], h2T_lo_ready)
                if has_a:
                    split_sums(g, b)
                if has_c:
                    finish(g - 2, b)
                if has_a:
                    dve.wait_ge(aH_hi_ready, g + 1)
                    lo_part(aH_lo[:, :], agg_a[:, :], aH_hi[:, :], aH_lo_ready)
                if has_b:
                    layer1_inputs(g - 1, 1 - b)
                if has_a:
                    dve.wait_ge(xb_ready, g + 1)
                    wait(dve, ln2_ready, g)
                    for k in range(C):
                        x1_max(g, b, k)
                    x1_stats(g, b, 3)
                if has_a:
                    dve.wait_ge(ln2_stats_done, 4 * g + 4)
                    nc.vector.memset(pause[:, 1:2], 0.0)
                    for k in range(C):
                        last = nc.vector.bn_aggr(moments2[:, k, :], stats2[:, k, :])
                    last.then_inc(ln2_moments, 1)

            nc.vector.memset(ones_r[:, :].bitcast(F32), 1.0)
            nc.vector.memset(hm[:, :, F + 1:WIDE], 0.0).then_inc(out_free[0], 16)
            nc.vector.memset(w1_full[:, F + 1:WIDE], 0.0).then_inc(out_free[1], 16)
            nc.vector.memset(sums_parts[:, :], 0.0)
            nc.vector.memset(pick[:, :], 0.0).then_inc(setup_dve, 1)
            dve.wait_ge(setup_dve, 1)
            nc.vector.memset(sums_parts[:, 16:17], 1.0)
            nc.vector.memset(sums_parts[:, 48:49], 1.0)
            step_k = P + 1
            for q, shift in ((0, 0), (32, C)):
                for c in (0, 8, 32):
                    at = shift + c
                    nc.vector.memset(pick[q:q + 32, at:at + (C - 1) * step_k + 1:step_k], 1.0)
            for c in (16, 48):
                last = nc.vector.memset(pick[64:P, c:c + (C - 1) * P + 1:P], 1.0)
            last.then_inc(setup_dve, 1)
            pre(0, 0)
            dve.wait_ge(setup_dve, 2)
            dve.wait_ge(sparse_loaded, 16 * SPARSE)
            nc.vector.tensor_scalar(pick[:, :], pick[:, :], edge_col[:, 0:1], None, ALU.mult).then_inc(setup_dve, 1)
            dve.wait_ge(small_loaded, 16 * SMALL)
            nc.vector.tensor_copy(b1_wide[:, :], b1_col[:, 0:1].to_broadcast([P, P])).then_inc(setup_dve, 1)
            dve.wait_ge(w0_loaded, 16 * len(SLOT_RUNS))
            w0_flat = w0_full[:, :, :].rearrange("p r o -> p (r o)")
            nc.vector.tensor_copy(w0_hi[:, :], w0_flat).then_inc(setup_dve, 1)
            dve.wait_ge(setup_dve, 5)
            nc.vector.tensor_tensor(w0_lo[:, :], w0_flat, w0_hi[:, :].bitcast(F32), ALU.subtract)
            dve.wait_ge(setup_pe, 1)
            nc.vector.tensor_copy(w1_full[:, 0:F], turn[1][:, 0:P])
            nc.vector.tensor_copy(w1_full[:, F:F + 1], agg_t[:, 1:2])
            nc.vector.tensor_copy(mask_cols[:, :], turn[1][:, P:P + G * C])
            nc.vector.tensor_copy(wa1_full[:, :], agg_t[:, 0:1].to_broadcast([P, P]))
            nc.vector.reduce_sum(kappa[:, :], agg_t[:, 2:4], AX.X).then_inc(setup_dve, 1)
            dve.wait_ge(setup_dve, 6)
            for q in (0, 32):
                last = nc.vector.tensor_tensor(bias_full[q:q + 1, F:F + 1], bias_full[q:q + 1, F:F + 1],
                                               kappa[q:q + 1, :], ALU.add)
            last.then_inc(setup_dve, 1)
            nc.vector.tensor_copy(w1_hi[:, :], w1_full[:, :])
            nc.vector.tensor_copy(wa1_hi[:, :], wa1_full[:, :])
            dve.wait_ge(setup_dve, 7)
            for j in range(2):
                last = nc.vector.tensor_copy(bias_r[:, j, :], bias_full[:, :])
            last.then_inc(setup_dve, 1)
            dve.wait_ge(setup_dve, 8)
            nc.vector.tensor_tensor(w1_lo[:, :], w1_full[:, :], w1_hi[:, :].bitcast(F32), ALU.subtract)
            nc.vector.tensor_tensor(wa1_lo[:, :], wa1_full[:, :], wa1_hi[:, :].bitcast(F32), ALU.subtract)
            for j in range(2):
                nc.vector.tensor_tensor(bias_r[32:64, j, :], bias_full[32:64, :], bias_r[32:64, j, :].bitcast(F32),
                                        ALU.subtract)
            for k in range(C):
                dve.wait_ge(setup_pe, k + 2)
                nc.vector.tensor_copy(c4[:, k, :], prod[k % 2][:, 0:RO]).then_inc(setup_dve, 1)
                dve.wait_ge(setup_dve, 9 + 2 * k)
                nc.vector.tensor_tensor(c4[32:64, k, :], prod[k % 2][32:64, 0:RO],
                                        c4[32:64, k, :].bitcast(F32), ALU.subtract).then_inc(setup_dve, 1)
            dve.wait_ge(setup_dve, 8 + 2 * C)
            nc.vector.engine_nop().then_inc(w_ready, 1)
            run(dve, step)

        @block.tensor
        def _(pe):
            def mm(dst, lhsT, rhs, start, stop):
                return nc.tensor.matmul(dst, lhsT, rhs, start=start, stop=stop)

            def turn_rows(dst, src, done):
                for k in range(C):
                    last = nc.tensor.transpose(dst[:, k * P:(k + 1) * P], src[:, k, :], ident[:, :])
                last.then_inc(done, 1)

            def turn_adj(b, m):
                for c in range(C):
                    last = nc.tensor.transpose(turn[1 - m % 2][:, c * P:(c + 1) * P],
                                               adj_sb[b][:, c, m * P:(m + 1) * P], ident[:, :])
                last.then_inc(adjT_done, 1)

            def aggregate(dst, hi, lo, k):
                mm(dst[:, :], h_hi[:, k, :], hi[:, k, :], k == 0, False)
                mm(dst[:, :], h_hi[:, k, :], lo[:, k, :], False, False)
                return mm(dst[:, :], h_lo[:, k, :], hi[:, k, :], False, k == C - 1)

            def times_w0(k, part, last_of_bank):
                hi, lo, c0, c1 = part
                nodes = slice(k * P, (k + 1) * P)
                dst = prod[k % 2][:, c0:c1]
                mm(dst, hi[:, nodes], w0_hi[:, c0:c1], False, False)
                mm(dst, hi[:, nodes], w0_lo[:, c0:c1], False, False)
                return mm(dst, lo[:, nodes], w0_hi[:, c0:c1], False, last_of_bank)

            H_PART = (hT_hi, hT_lo, 4 * F, 7 * F)
            ATH_PART = (atH_hi, atH_lo, 2 * F, 4 * F)
            AH_PART = (aH_hi, aH_lo, 0, 2 * F)

            def relations(g, k):
                mm(prod[k % 2][:, 0:BANK], sumsT[:, :], c4[:, k, 0:BANK], True, False)
                mm(prod[k % 2][:, BANK:RO], sumsT[:, :], c4[:, k, BANK:RO], True, False)
                times_w0(k, H_PART, True)
                times_w0(k, ATH_PART, False)
                if k == 0:
                    pe.wait_ge(aH_lo_ready, g + 1)
                times_w0(k, AH_PART, True).then_inc(prod_done, 1)

            def attend(i):
                for j in range(C):
                    last = mm(prod[0][:, 256 * i:256 * i + WIDE], att[:, j, i * P:(i + 1) * P],
                              hm[:, j, :], j == 0, j == C - 1)
                last.then_inc(att_done, 1)

            def step(g, b, has_pre=True, has_a=True, has_b=True, has_c=True):
                if has_a:
                    pe.wait_ge(h_ready, g + 1)
                    wait(pe, sumsT_ready, g)
                    turn_rows(turn[0], h, hT_done)
                    pe.wait_ge(h_lo_ready, g + 1)
                    pe.wait_ge(adj_lo_ready, 4 * g + 2)
                    wait(pe, sig_ready, 4 * g - 4)
                    aggregate(agg_t, adj_hi[b], adj_lo[b], 0)
                    aggregate(agg_t, adj_hi[b], adj_lo[b], 1)
                    wait(pe, h2T_lo_ready, g - 1)
                    turn_adj(b, 0)
                    pe.wait_ge(adj_lo_ready, 4 * g + 4)
                    aggregate(agg_t, adj_hi[b], adj_lo[b], 2)
                    aggregate(agg_t, adj_hi[b], adj_lo[b], 3).then_inc(atH_done, 1)
                    pe.wait_ge(hT_lo_ready, g + 1)
                    turn_adj(b, 1)
                    pe.wait_ge(adjT_ready, 4 * g + 1)
                    turn_adj(b, 2)
                if has_c:
                    pe.wait_ge(hm_ready, g - 1)
                    pe.wait_ge(att_ready, 4 * g - 4)
                    if has_b:
                        pe.wait_ge(max_done, 4 * g - 1)
                    else:
                        pe.wait_ge(out_ready, g - 2)
                    attend(0)
                if has_a:
                    pe.wait_ge(adjT_ready, 4 * g + 2)
                    turn_adj(b, 3)
                if has_c:
                    for i in range(1, C):
                        attend(i)
                if has_b:
                    pe.wait_ge(h2_ready, g)
                    if has_a:
                        pe.wait_ge(adjT_ready, 4 * g + 3)
                    turn_rows(turn[1], h2, h2T_done)
                if has_a:
                    wait(pe, aH_lo_ready, g)
                    for k in range(C):
                        pe.wait_ge(adjT_lo_ready, 4 * g + k + 1)
                        last = aggregate(agg_a, adjT_hi, adjT_lo, k)
                    last.then_inc(aH_done, 1)
                if has_b:
                    pe.wait_ge(h2T_lo_ready, g)
                    if has_a:
                        pe.wait_ge(atH_lo_ready, g + 1)
                    mm(agg_t[:, :], wa1_hi[:, :], h2T_hi[:, :], True, False)
                    mm(agg_t[:, :], wa1_hi[:, :], h2T_lo[:, :], False, False)
                    mm(agg_t[:, :], wa1_lo[:, :], h2T_hi[:, :], False, True).then_inc(s1_done, 1)
                if has_a:
                    pe.wait_ge(sums_ready, g + 1)
                    pe.wait_ge(adjT_ready, 4 * g + 4)
                    nc.tensor.transpose(turn[0][:, 0:P], sums_parts[:, :], ident[:, :]).then_inc(sumsT_done, 1)
                if has_b:
                    pe.wait_ge(max_done, 4 * g)
                    for j in range(C):
                        dst = prod[1][:, 256 * j:256 * j + WIDE]
                        nodes = slice(j * P, (j + 1) * P)
                        if j % 2 == 0:
                            mm(prod[1][:, 256 * j:256 * j + 512].rearrange("p (j w) -> p j w", j=2)[:, :, 0:WIDE],
                               ones_r[:, :], bias_r[:, :, :], True, False)
                        mm(dst, h2T_hi[:, nodes], w1_hi[:, :], False, False)
                        mm(dst, h2T_hi[:, nodes], w1_lo[:, :], False, False)
                        last = mm(dst, h2T_lo[:, nodes], w1_hi[:, :], False, j % 2 == 1)
                    last.then_inc(hw_done, 1)
                if has_a:
                    pe.wait_ge(sumsT_ready, g + 1)
                    for k in range(C):
                        if k == 0 and has_c:
                            pe.wait_ge(out_ready, g - 1)
                        elif k == 1 and has_b:
                            pe.wait_ge(hm_ready, g)
                        elif k >= 2:
                            pe.wait_ge(max_done, 4 * g + k - 1)
                        relations(g, k)

            pe.wait_ge(ident_ready, 1)
            pe.wait_ge(small_loaded, 16 * SMALL)
            pe.wait_ge(setup_dve, 4)
            nc.tensor.transpose(turn[1][:, 0:P], w1_nat[:, :], ident[:, :])
            nc.tensor.transpose(turn[1][:, P:P + G * C], mask_rows[:, :], ident[0:G * C, 0:G * C])
            mm(agg_t[:, 0:2], w1_nat[:, :], a_cols[:, :], True, True)
            mm(agg_t[:, 2:4], b1_wide[:, :], a_cols[:, :], True, True).then_inc(setup_pe, 1)
            for k in range(C):
                if k >= 2:
                    pe.wait_ge(setup_dve, 8 + 2 * (k - 1))
                mm(prod[k % 2][:, 0:BANK], pick[:, k * P:(k + 1) * P], wrel[:, 0:BANK], True, True)
                mm(prod[k % 2][:, BANK:RO], pick[:, k * P:(k + 1) * P], wrel[:, BANK:RO], True, True)\
                    .then_inc(setup_pe, 1)
            pe.wait_ge(w_ready, 1)
            run(pe, step)


_INS = ['x', 'adj', 'nodemask', 'L0_gnn_W', 'L0_gnn_W_edges', 'L0_gnn_b', 'L1_gnn_W', 'L1_gnn_b', 'L1_gnn_a1',
        'L1_gnn_a2', 'L1_gnn_att_b']


def kernel(**inputs):
    import numpy as _np
    import concourse.bacc as _bacc
    from concourse import mybir as _mybir
    from concourse.bass_utils import run_bass_kernel_spmd as _run

    nc = _bacc.Bacc("TRN2", target_bir_lowering=False, num_devices=1)
    arrays, args = {}, []
    for name in _INS:
        a = _np.ascontiguousarray(inputs[name])
        if name == 'L1_gnn_att_b':
            a = a.reshape(1, 1)
        arrays[f"in_{name}_dram"] = a
        args.append(nc.dram_tensor(f"in_{name}_dram", a.shape, _mybir.dt.from_np(a.dtype), kind="ExternalInput").ap())
    shape = inputs['x'].shape
    args.append(nc.dram_tensor("out_0_dram", shape, _mybir.dt.float32, kind="ExternalOutput").ap())
    build(nc, *args)
    r = _run(nc, [arrays], core_ids=[0])
    return r.results[0]["out_0_dram"]
```

```python
from contextlib import ExitStack

import concourse.bass as bass
from concourse import mybir

F32 = mybir.dt.float32
F32R = mybir.dt.float32r
ALU = mybir.AluOpType
ACT = mybir.ActivationFunctionType
AX = mybir.AxisListType
P = 128
LN_EPS = 1e-5
DEN_EPS = 1e-8
SLOTS = (0, 1, 3, 4, 2, 5, 6)
SLOT_RUNS = ((0, 0, 2), (2, 3, 2), (4, 2, 1), (5, 5, 2))


def build(nc, x, adj, nodemask, w0, w_edges, b0, w1, b1, a1, a2, att_b, out):
    G, N, F = x.shape
    R, D = w_edges.shape
    C = N // P
    RO = R * F
    BANK = 512
    WIDE = F + 1
    assert F == P and R == 7 and C == 4 and N == BANK and G % 2 == 0 and R * D <= P

    x_d = x.rearrange("g (c p) f -> g p c f", p=P)
    adj_d = adj.rearrange("g (c p) n -> g p c n", p=P)
    out_d = out.rearrange("g (c p) f -> g p c f", p=P)

    with ExitStack() as ctx:
        def sb(name, shape, dt=F32):
            return ctx.enter_context(nc.sbuf_tensor(name, shape, dt))

        def ps(name, cols):
            return ctx.enter_context(nc.psum_tensor(name, [P, cols], F32))

        def sem(name):
            return ctx.enter_context(nc.semaphore(name))

        ident = sb("ident", [P, P])
        ones = sb("ones", [P, P])
        w0_full = sb("w0_full", [P, R, F])
        w0_hi = sb("w0_hi", [P, RO], F32R)
        w0_lo = sb("w0_lo", [P, RO], F32R)
        wrel = sb("wrel", [P, RO])
        edge_col = sb("edge_col", [P, 1])
        pick = sb("pick", [P, P])
        c_rows = sb("c_rows", [P, RO], F32R)
        chunk_rows = sb("chunk_rows", [P, C])
        chunk_rows_lo = sb("chunk_rows_lo", [P, C])
        w1_nat = sb("w1_nat", [P, P])
        a_cols = sb("a_cols", [P, 2])
        b1_col = sb("b1_col", [P, 1])
        b1_wide = sb("b1_wide", [P, P])
        w1_full = sb("w1_full", [P, WIDE])
        wa1_full = sb("wa1_full", [P, P])
        wa1_hi = sb("wa1_hi", [P, P], F32R)
        wa1_lo = sb("wa1_lo", [P, P], F32R)
        kappa = sb("kappa", [P, 1])
        att_b_col = sb("att_b_col", [P, 1])
        b1_rows = sb("b1_rows", [P, P])
        b0_sb = sb("b0_sb", [P, C, F])
        mask_rows = sb("mask_rows", [G * C, P])
        mask_cols = sb("mask_cols", [P, G * C])
        ln_eps = sb("ln_eps", [P, C])
        minus_half = sb("minus_half", [P, C])
        minus_one = sb("minus_one", [P, C])

        x_sb = [sb(f"x_sb{i}", [P, C, F]) for i in range(2)]
        adj_sb = [sb(f"adj_sb{i}", [P, C, N]) for i in range(2)]
        adjT = [sb(f"adjT{i}", [P, C, N]) for i in range(2)]
        xb = [sb(f"xb{i}", [P, C, F]) for i in range(2)]
        x1 = [sb(f"x1_{i}", [P, C, F]) for i in range(2)]
        out_sb = [sb(f"out_sb{i}", [P, C, F]) for i in range(2)]
        h = sb("h", [P, C, F])
        h_hi = sb("h_hi", [P, C, F], F32R)
        h_lo = sb("h_lo", [P, C, F], F32R)
        adj_hi = [sb(f"adj_hi{i}", [P, C, N], F32R) for i in range(2)]
        adj_lo = [sb(f"adj_lo{i}", [P, C, N], F32R) for i in range(2)]
        adjT_hi = sb("adjT_hi", [P, C, N], F32R)
        adjT_lo = sb("adjT_lo", [P, C, N], F32R)
        stats = sb("stats", [P, C, 6])
        stats2 = sb("stats2", [P, C, 6])
        moments1 = sb("moments1", [P, C, 2])
        moments2 = sb("moments2", [P, C, 2])
        ln1 = {n: sb(f"ln1_{n}", [P, C]) for n in ("var", "scale", "neg", "shift")}
        ln2 = {n: sb(f"ln2_{n}", [P, C]) for n in ("var", "scale", "neg", "shift")}
        hT_hi = sb("hT_hi", [P, N], F32R)
        hT_lo = sb("hT_lo", [P, N], F32R)
        atH_hi = sb("atH_hi", [P, N], F32R)
        atH_lo = sb("atH_lo", [P, N], F32R)
        aH_hi = sb("aH_hi", [P, N], F32R)
        aH_lo = sb("aH_lo", [P, N], F32R)
        sums = [sb(f"sums{i}", [P, 2 * C]) for i in range(2)]
        sums_parts = sb("sums_parts", [P, P])
        sumsT = sb("sumsT", [P, C, P], F32R)
        mx = sb("mx", [P, C, F])
        pause = sb("pause", [P, 2])
        pause_act = sb("pause_act", [P, 1])
        h2 = sb("h2", [P, C, F])
        h2T = sb("h2T", [P, N])
        h2T_hi = sb("h2T_hi", [P, N], F32R)
        h2T_lo = sb("h2T_lo", [P, N], F32R)
        m_cur = [sb(f"m_cur{i}", [P, C]) for i in range(2)]
        s2 = sb("s2", [P, C])
        raw = sb("raw", [P, C, WIDE])
        values = sb("values", [P, C, WIDE])
        sig = sb("sig", [P, C, N])
        att = sb("att", [P, C, N])
        den = sb("den", [P, C])
        den_eps = sb("den_eps", [P, C])
        den_inv = sb("den_inv", [P, C])
        m_sq = sb("m_sq", [P, C])
        row_scale = sb("row_scale", [P, C])

        prod = [ps(f"prod{i}", 2 * BANK) for i in range(2)]
        turn = [ps(f"turn{i}", BANK) for i in range(2)]
        agg_t = ps("agg_t", BANK)
        agg_a = ps("agg_a", BANK)

        x_loaded = [sem(f"x_loaded{i}") for i in range(2)]
        adj_loaded = [sem(f"adj_loaded{i}") for i in range(2)]
        out_free = [sem(f"out_free{i}") for i in range(2)]
        ln1_stats_done = sem("ln1_stats_done")
        ln1_moments = sem("ln1_moments")
        ln1_pool = sem("ln1_pool")
        ln1_ready = sem("ln1_ready")
        h_ready = sem("h_ready")
        h_steps = sem("h_steps")
        h_half_ready = sem("h_half_ready")
        xb_ready = sem("xb_ready")
        hT_done = sem("hT_done")
        hT_hi_ready = sem("hT_hi_ready")
        hT_lo_ready = sem("hT_lo_ready")
        adjT_done = sem("adjT_done")
        adjT_ready = sem("adjT_ready")
        adj_hi_ready = sem("adj_hi_ready")
        adj_lo_ready = sem("adj_lo_ready")
        adjT_hi_ready = sem("adjT_hi_ready")
        adjT_lo_ready = sem("adjT_lo_ready")
        h_hi_ready = sem("h_hi_ready")
        h_lo_ready = sem("h_lo_ready")
        atH_done = sem("atH_done")
        atH_hi_ready = sem("atH_hi_ready")
        atH_lo_ready = sem("atH_lo_ready")
        aH_done = sem("aH_done")
        aH_hi_ready = sem("aH_hi_ready")
        aH_lo_ready = sem("aH_lo_ready")
        sums_hi_done = sem("sums_hi_done")
        sums_ready = sem("sums_ready")
        sumsT_done = sem("sumsT_done")
        sumsT_ready = sem("sumsT_ready")
        prod_done = sem("prod_done")
        max_done = sem("max_done")
        x1_ready = sem("x1_ready")
        ln2_stats_done = sem("ln2_stats_done")
        ln2_moments = sem("ln2_moments")
        ln2_pool = sem("ln2_pool")
        ln2_ready = sem("ln2_ready")
        h2_ready = sem("h2_ready")
        h2_steps = sem("h2_steps")
        h2_half_ready = sem("h2_half_ready")
        h2T_done = sem("h2T_done")
        h2T_ready = sem("h2T_ready")
        h2T_hi_ready = sem("h2T_hi_ready")
        h2T_lo_ready = sem("h2T_lo_ready")
        s1_done = sem("s1_done")
        hw_done = sem("hw_done")
        s2_ready = sem("s2_ready")
        raw_ready = sem("raw_ready")
        values_ready = sem("values_ready")
        sig_ready = sem("sig_ready")
        att_ready = sem("att_ready")
        att_done = sem("att_done")
        scale_steps = sem("scale_steps")
        out_ready = sem("out_ready")
        ones_ready = sem("ones_ready")
        zeroed = sem("zeroed")
        ident_zero = sem("ident_zero")
        ident_ready = sem("ident_ready")
        w0_loaded = sem("w0_loaded")
        small_loaded = sem("small_loaded")
        sparse_loaded = sem("sparse_loaded")
        b0_loaded = sem("b0_loaded")
        pick_steps = sem("pick_steps")
        w0_hi_ready = sem("w0_hi_ready")
        w0_ready = sem("w0_ready")
        row_steps = sem("row_steps")
        rows_ready = sem("rows_ready")
        c_done = sem("c_done")
        c_hi_ready = sem("c_hi_ready")
        c_ready = sem("c_ready")
        b1_ready = sem("b1_ready")
        w1_done = sem("w1_done")
        w1_taken = sem("w1_taken")
        wa1_hi_ready = sem("wa1_hi_ready")
        w1_ready = sem("w1_ready")

        block = ctx.enter_context(nc.Block())

        def wait(eng, s, value):
            if not isinstance(value, int) or value > 0:
                eng.wait_ge(s, value)

        def loads(g, i):
            return 8 * (g - i) + 16

        def run(eng, step):
            def peeled(g):
                step(g, g % 2, has_pre=g < G - 1, has_a=g < G, has_b=1 <= g <= G, has_c=g >= 2, first=g == 0)

            for g in range(3):
                peeled(g)
            with eng.Fori(0, (G - 4) // 2) as i:
                step(2 * i + 3, 1)
                step(2 * i + 4, 0)
            for g in range(G - 1, G + 2):
                peeled(g)

        def shared(has_a, has_c):
            return not (has_a and has_c)

        SMALL = 6
        SPARSE = R + len(SLOT_RUNS)

        @block.sync
        def _(sp):
            def load_x(g, i):
                wait(sp, ln1_moments, g - 1)
                wait(sp, h_ready, g - 1)
                wait(sp, xb_ready, g - 1)
                sp.dma_start(x_sb[i][:, :, :], x_d[g]).then_inc(x_loaded[i], 16)

            def load_adj(g, i):
                used = 4 * g - 4 if isinstance(g, int) else sp.snap(4 * g - 4)
                wait(sp, adj_hi_ready, used)
                wait(sp, adj_lo_ready, used)
                wait(sp, adjT_done, used)
                sp.dma_start(adj_sb[i][:, :, :], adj_d[g]).then_inc(adj_loaded[i], 16)

            def store(g, i):
                sp.wait_ge(out_ready, 2 * g + 2)
                sp.dma_start(out_d[g], out_sb[i][:, :, :]).then_inc(out_free[i], 16)

            def step(g, b, load=True, done=True):
                if load:
                    load_x(g + 2, b)
                    load_adj(g + 2, b)
                if done:
                    store(g - 2, b)

            sp.dma_start(x_sb[0][:, :, :], x_d[0]).then_inc(x_loaded[0], 16)
            sp.dma_start(adj_sb[0][:, :, :], adj_d[0]).then_inc(adj_loaded[0], 16)
            sp.dma_start(adj_sb[1][:, :, :], adj_d[1]).then_inc(adj_loaded[1], 16)
            sp.wait_ge(zeroed, 1)
            for s, r, n in SLOT_RUNS:
                sp.dma_start(edge_col[s * D:(s + n) * D, 0:1],
                             w_edges[r:r + n, :].rearrange("r (d a) -> (r d) a", a=1)).then_inc(sparse_loaded, 16)
            for s, r in enumerate(SLOTS):
                sp.dma_start(wrel[s * D:(s + 1) * D, s * F:(s + 1) * F], w0[r, F:F + D, :]).then_inc(sparse_loaded, 16)
            for s, r, n in SLOT_RUNS:
                sp.dma_start(w0_full[:, s:s + n, :],
                             w0[r:r + n, 0:F, :].rearrange("r f o -> f r o")).then_inc(w0_loaded, 16)
            sp.dma_start(x_sb[1][:, :, :], x_d[1]).then_inc(x_loaded[1], 16)
            sp.dma_start(b0_sb[:, :, :], b0.rearrange("(c p) f -> p c f", p=P)).then_inc(b0_loaded, 16)
            sp.dma_start(w1_nat[:, :], w1).then_inc(small_loaded, 16)
            sp.dma_start(a_cols[:, 0:1], a1.rearrange("(p a) -> p a", a=1)).then_inc(small_loaded, 16)
            sp.dma_start(a_cols[:, 1:2], a2.rearrange("(p a) -> p a", a=1)).then_inc(small_loaded, 16)
            sp.dma_start(b1_col[:, :], b1.rearrange("(p a) -> p a", a=1)).then_inc(small_loaded, 16)
            sp.dma_start(mask_rows[:, :], nodemask.rearrange("g (c p) -> (g c) p", p=P)).then_inc(small_loaded, 16)
            sp.dma_start(att_b_col[0:1, :], att_b).then_inc(small_loaded, 16)
            step(0, 0, done=False)
            step(1, 1, done=False)
            with sp.Fori(0, (G - 4) // 2) as i:
                step(2 * i + 2, 0)
                step(2 * i + 3, 1)
            for g in range(G - 2, G + 2):
                step(g, g % 2, load=False)
            for i in range(2):
                sp.wait_ge(out_free[i], 8 * G + 16)

        @block.gpsimd
        def _(pool):
            def norm(t, moments, moments_ready, steps_done, ready, g):
                pool.wait_ge(moments_ready, g + 1)
                nc.gpsimd.tensor_tensor(t["var"][:, :], moments[:, :, 1], ln_eps[:, :],
                                        ALU.add).then_inc(steps_done, 1)
                nc.gpsimd.tensor_tensor(t["neg"][:, :], moments[:, :, 0], minus_one[:, :],
                                        ALU.mult).then_inc(steps_done, 1)
                pool.wait_ge(steps_done, 3 * g + 2)
                nc.gpsimd.tensor_tensor(t["scale"][:, :], t["var"][:, :], minus_half[:, :],
                                        ALU.pow).then_inc(steps_done, 1)
                pool.wait_ge(steps_done, 3 * g + 3)
                nc.gpsimd.tensor_tensor(t["shift"][:, :], t["neg"][:, :], t["scale"][:, :],
                                        ALU.mult).then_inc(ready, 1)

            def pre(g, i):
                wait(pool, h_ready, g)
                norm(ln1, moments1, ln1_moments, ln1_pool, ln1_ready, g)
                add_b0(g, i)

            def add_b0(g, i):
                wait(pool, x1_ready, 4 * g - 4)
                pool.wait_ge(x_loaded[i], loads(g, i))
                nc.gpsimd.tensor_tensor(xb[i][:, :, :], x_sb[i][:, :, :], b0_sb[:, :, :],
                                        ALU.add).then_inc(xb_ready, 1)

            def split_adj(g, i, ks):
                wait(pool, atH_done, g - 1)
                for k in ks:
                    pool.wait_ge(adj_hi_ready, 4 * g + k + 1)
                    nc.gpsimd.tensor_tensor(adj_lo[i][:, k, :], adj_sb[i][:, k, :], adj_hi[i][:, k, :].bitcast(F32),
                                            ALU.subtract).then_inc(adj_lo_ready, 1)

            def split_h(g):
                pool.wait_ge(h_hi_ready, g + 1)
                nc.gpsimd.tensor_tensor(h_lo[:, :, :], h[:, :, :], h_hi[:, :, :].bitcast(F32),
                                        ALU.subtract).then_inc(h_lo_ready, 1)

            def attention(g, i):
                wait(pool, att_done, 4 * g)
                for j in range(C):
                    pool.wait_ge(sig_ready, 4 * g + j + 1)
                    nc.gpsimd.tensor_tensor(att[:, j, :], sig[:, j, :], adjT[i][:, j, :],
                                            ALU.mult).then_inc(att_ready, 1)

            def mask_values(g, i):
                pool.wait_ge(raw_ready, g + 1)
                wait(pool, att_done, 4 * g)
                nc.gpsimd.tensor_tensor(values[:, :, :], raw[:, :, :],
                                        m_cur[i][:, :].unsqueeze(2).to_broadcast([P, C, WIDE]),
                                        ALU.mult).then_inc(values_ready, 1)

            def step(g, b, has_pre=True, has_a=True, has_b=True, has_c=True, first=False):
                if has_b:
                    wait(pool, h2_ready, g - 1)
                    if isinstance(g, int) and g == 2:
                        pool.wait_ge(h2_half_ready, 1)
                    norm(ln2, moments2, ln2_moments, ln2_pool, ln2_ready, g - 1)
                if has_pre:
                    pre(g + 1, 1 - b)
                    split_adj(g + 1, 1 - b, (0, 1, 2, 3))
                if has_b and (has_pre or not has_a):
                    mask_values(g - 1, 1 - b)
                if has_pre:
                    split_h(g + 1)
                if has_b and has_a:
                    attention(g - 1, 1 - b)

            nc.gpsimd.memset(ident[:, :], 0.0).then_inc(ident_zero, 1)
            nc.gpsimd.memset(wrel[:, :], 0.0)
            nc.gpsimd.memset(att_b_col[:, :], 0.0)
            nc.gpsimd.memset(edge_col[:, :], 0.0).then_inc(zeroed, 1)
            pool.wait_ge(ident_zero, 1)
            nc.gpsimd.affine_select(out=ident[:, :], in_=ident[:, :], compare_op=ALU.not_equal, fill=1.0, base=0,
                                    pattern=[[-1, P]], channel_multiplier=1).then_inc(ident_ready, 1)
            nc.gpsimd.memset(ln_eps[:, :], LN_EPS)
            nc.gpsimd.memset(minus_half[:, :], -0.5)
            nc.gpsimd.memset(minus_one[:, :], -1.0).then_inc(ident_zero, 1)
            pool.wait_ge(ident_zero, 2)
            norm(ln1, moments1, ln1_moments, ln1_pool, ln1_ready, 0)
            split_h(0)
            pool.wait_ge(b0_loaded, 16)
            add_b0(0, 0)
            pool.wait_ge(w0_hi_ready, 1)
            nc.gpsimd.tensor_tensor(w0_lo[:, :], w0_full[:, :, :].rearrange("p r o -> p (r o)"),
                                    w0_hi[:, :].bitcast(F32), ALU.subtract).then_inc(w0_ready, 1)
            pool.wait_ge(adj_lo_ready, 4)
            run(pool, step)

        @block.scalar
        def _(act):
            def apply_norm(t, src, dst, done, ks=range(C)):
                for k in ks:
                    last = nc.scalar.activation(dst[:, k, :], src[:, k, :], ACT.Relu,
                                                bias=t["shift"][:, k:k + 1], scale=t["scale"][:, k:k + 1])
                last.then_inc(done, 1)

            def split_adj(g, i, ks):
                act.wait_ge(adj_loaded[i], loads(g, i))
                wait(act, atH_done, g - 1)
                wait(act, sums_ready, g - 1)
                for k in ks:
                    nc.scalar.activation(adj_hi[i][:, k, :], adj_sb[i][:, k, :], ACT.Copy,
                                         accum_out=sums[i][:, k:k + 1]).then_inc(adj_hi_ready, 1)

            def take_adjT(g, b, m):
                wait(act, att_ready, 4 * (g - 2) + m + 1)
                act.wait_ge(adjT_done, 4 * g + m + 1)
                nc.scalar.activation(adjT[b][:, m, :], turn[1 - m % 2][:, :], ACT.Copy,
                                     accum_out=sums[b][:, C + m:C + m + 1]).then_inc(adjT_ready, 1)

            def hi_part(dst, src, ready):
                nc.scalar.activation(dst, src, ACT.Copy).then_inc(ready, 1)

            def split_h(g):
                act.wait_ge(h_ready, g + 1)
                wait(act, aH_done, g)
                hi_part(h_hi[:, :, :], h[:, :, :], h_hi_ready)

            def norm1(g, i, ks=range(C)):
                act.wait_ge(ln1_ready, g + 1)
                wait(act, hT_done, g)
                wait(act, h_lo_ready, g)
                apply_norm(ln1, x_sb[i], h, h_ready, ks)

            def split_adjT(g, b, m):
                hi_part(adjT_hi[:, m, :], adjT[b][:, m, :], adjT_hi_ready)

            def take_sumsT(k):
                nc.scalar.activation(sumsT[:, k, :], turn[0][:, 0:P], ACT.Copy,
                                     scale=chunk_rows[:, k:k + 1]).then_inc(sumsT_ready, 1)

            def norm2(g, i, ks):
                act.wait_ge(ln2_ready, g + 1)
                wait(act, h2T_done, g)
                apply_norm(ln2, x1[i], h2, h2_ready, ks)

            def step(g, b, has_pre=True, has_a=True, has_b=True, has_c=True, first=False):
                if has_a:
                    act.wait_ge(hT_done, g + 1)
                    hi_part(hT_hi[:, :], turn[0][:, :], hT_hi_ready)
                if has_pre and not first:
                    split_adj(g + 1, 1 - b, (0,))
                if has_a:
                    take_adjT(g, b, 0)
                if first:
                    split_adj(g + 1, 1 - b, (0, 1, 2, 3))
                if has_a:
                    take_adjT(g, b, 1)
                    wait(act, aH_done, g)
                    act.wait_ge(adjT_ready, 4 * g + 1)
                    split_adjT(g, b, 0)
                if has_b and not has_c:
                    norm2(g - 1, 1 - b, (0, 1))
                if has_a:
                    take_adjT(g, b, 2)
                    act.wait_ge(adjT_ready, 4 * g + 2)
                    split_adjT(g, b, 1)
                if has_b and (has_c or not has_a):
                    norm2(g - 1, 1 - b, range(C) if has_a else (0, 1))
                if has_a:
                    take_adjT(g, b, 3)
                    act.wait_ge(adjT_ready, 4 * g + 4)
                    split_adjT(g, b, 2)
                    split_adjT(g, b, 3)
                if has_b:
                    act.wait_ge(h2T_done, g)
                    wait(act, hw_done, g - 1)
                    nc.scalar.activation(h2T[:, :], turn[1][:, :], ACT.Copy).then_inc(h2T_ready, 1)
                    hi_part(h2T_hi[:, :], turn[1][:, :], h2T_hi_ready)
                if has_a:
                    act.wait_ge(atH_done, g + 1)
                    hi_part(atH_hi[:, :], agg_t[:, :], atH_hi_ready)
                if first:
                    act.wait_ge(c_done, 1)
                    hi_part(c_rows[:, :], prod[0][:, 0:RO], c_hi_ready)
                if has_pre and not first:
                    split_adj(g + 1, 1 - b, (1, 2, 3))
                if has_a:
                    if first:
                        act.wait_ge(rows_ready, 1)
                    act.wait_ge(sumsT_done, g + 1)
                    take_sumsT(0)
                    act.wait_ge(aH_done, g + 1)
                    hi_part(aH_hi[:, :], agg_a[:, :], aH_hi_ready)
                    for k in range(1, C):
                        take_sumsT(k)
                if has_pre:
                    norm1(g + 1, 1 - b)
                    split_h(g + 1)
                if has_b:
                    act.wait_ge(s1_done, g)
                    act.wait_ge(s2_ready, g)
                    wait(act, att_ready, 4 * g - 4)
                    for j in range(C):
                        nc.scalar.activation(sig[:, j, :], agg_t[:, :], ACT.Sigmoid,
                                             bias=s2[:, j:j + 1]).then_inc(sig_ready, 1)
                if has_b and has_a and not has_pre:
                    act.wait_ge(raw_ready, g)
                    act.wait_ge(att_done, 4 * g - 4)
                    for j in range(C):
                        last = nc.scalar.activation(values[:, j, :], raw[:, j, :], ACT.Copy,
                                                    scale=m_cur[1 - b][:, j:j + 1])
                    last.then_inc(values_ready, 1)

            act.wait_ge(ones_ready, 1)
            nc.scalar.activation(pause_act[:, :], ones[:, 0:1], ACT.Sigmoid)
            act.wait_ge(x_loaded[0], 16)
            norm1(0, 0, (0, 1))
            act.wait_ge(h_half_ready, 1)
            split_h(0)
            split_adj(0, 0, (0, 1, 2, 3))
            run(act, step)

        @block.vector
        def _(dve):
            hw = prod[1][:, :].rearrange("p (j w) -> p j w", j=C)

            def lo_part(dst, src, hi, ready):
                nc.vector.tensor_tensor(dst, src, hi.bitcast(F32), ALU.subtract).then_inc(ready, 1)

            def pre(g, i):
                dve.wait_ge(x_loaded[i], loads(g, i))
                for k in range(C):
                    last = nc.vector.bn_stats(stats[:, k, :], x_sb[i][:, k, :])
                last.then_inc(ln1_stats_done, 1)
                dve.wait_ge(ln1_stats_done, g + 1)
                wait(dve, ln1_ready, g)
                nc.vector.memset(pause[:, 0:1], 0.0)
                for k in range(C):
                    last = nc.vector.bn_aggr(moments1[:, k, :], stats[:, k, :])
                last.then_inc(ln1_moments, 1)

            def attention_term(g):
                dve.wait_ge(hw_done, g + 1)
                wait(dve, sig_ready, 4 * g)
                nc.vector.tensor_tensor(s2[:, :], hw[:, :, F], kappa[:, 0:1].to_broadcast([P, C]),
                                        ALU.add).then_inc(s2_ready, 1)

            def raw_values(g):
                dve.wait_ge(hw_done, g + 1)
                wait(dve, values_ready, g)
                nc.vector.tensor_tensor(raw[:, :, 0:F], hw[:, :, 0:F],
                                        b1_rows[:, :].unsqueeze(1).to_broadcast([P, C, F]),
                                        ALU.add).then_inc(raw_ready, 1)

            def results(g):
                if isinstance(g, int) and g == G - 1:
                    return [(2 * t, 2 * t + 2, prod[t][:, :].rearrange("p (j w) -> p j w", j=2)) for t in range(2)]
                return [(0, C, prod[0][:, :].rearrange("p (j w) -> p j w", j=C))]

            def scale_step(g, i, n):
                if n == 0:
                    dve.wait_ge(out_free[i], loads(g, i))
                    nc.vector.tensor_tensor(m_sq[:, :], m_cur[i][:, :], m_cur[i][:, :], ALU.mult)
                    dve.wait_ge(att_done, 4 * g + 4)
                    for k0, k1, res in results(g):
                        last = nc.vector.tensor_tensor(den[:, k0:k1], res[:, :, F], m_cur[i][:, k0:k1], ALU.mult)
                if n > 0:
                    dve.wait_ge(scale_steps, 4 * g + n)
                if n == 1:
                    last = nc.vector.tensor_scalar(den_eps[:, :], den[:, :], DEN_EPS, None, ALU.add)
                if n == 2:
                    last = nc.vector.reciprocal(den_inv[:, :], den_eps[:, :])
                if n == 3:
                    last = nc.vector.tensor_tensor(row_scale[:, :], den_inv[:, :], m_sq[:, :], ALU.mult)
                last.then_inc(scale_steps, 1)

            def finish(g, i):
                dve.wait_ge(scale_steps, 4 * g + 4)
                for k0, k1, res in results(g):
                    for k in range(k0, k1):
                        last = nc.vector.scalar_tensor_tensor(out_sb[i][:, k, :], res[:, k - k0, 0:F],
                                                              row_scale[:, k:k + 1], x1[i][:, k, :],
                                                              ALU.mult, ALU.add)
                        if k % 2 == 1:
                            last.then_inc(out_ready, 1)

            def last_attention(g, i):
                for j in range(C):
                    dve.wait_ge(sig_ready, 4 * g + j + 1)
                    if j == 0:
                        dve.wait_ge(att_done, 4 * g)
                    nc.vector.tensor_tensor(att[:, j, :], sig[:, j, :], adjT[i][:, j, :],
                                            ALU.mult).then_inc(att_ready, 1)

            def split_adjT(g, b, m):
                dve.wait_ge(adjT_hi_ready, 4 * g + m + 1)
                lo_part(adjT_lo[:, m, :], adjT[b][:, m, :], adjT_hi[:, m, :], adjT_lo_ready)

            def split_sums(g, b):
                dve.wait_ge(adj_hi_ready, 4 * g + 4)
                dve.wait_ge(adjT_ready, 4 * g + 4)
                wait(dve, sumsT_done, g)
                nc.vector.tensor_copy(sums_parts[:, 0:2 * C].bitcast(F32R), sums[b][:, :])
                nc.vector.tensor_copy(sums_parts[:, 32:32 + 2 * C].bitcast(F32R), sums[b][:, :])\
                    .then_inc(sums_hi_done, 1)
                dve.wait_ge(sums_hi_done, g + 1)
                nc.vector.tensor_tensor(sums_parts[:, 2 * C:4 * C].bitcast(F32R), sums[b][:, :],
                                        sums_parts[:, 0:2 * C], ALU.subtract).then_inc(sums_ready, 1)

            def x1_max(g, b, k):
                dve.wait_ge(prod_done, 4 * g + k + 1)
                nc.vector.tensor_reduce(mx[:, k, :], prod[k % 2][:, 0:RO].rearrange("p (r o) -> p o r", r=R),
                                        AX.X, ALU.max).then_inc(max_done, 1)
                if k > 0:
                    x1_stats(g, b, k - 1)
                dve.wait_ge(max_done, 4 * g + k + 1)
                nc.vector.tensor_tensor(x1[b][:, k, :], mx[:, k, :], xb[b][:, k, :], ALU.add).then_inc(x1_ready, 1)

            def x1_moments(g, b):
                x1_stats(g, b, 3)
                wait(dve, ln2_ready, g)
                dve.wait_ge(ln2_stats_done, 4 * g + 4)
                nc.vector.memset(pause[:, 1:2], 0.0)
                for k in range(C):
                    last = nc.vector.bn_aggr(moments2[:, k, :], stats2[:, k, :])
                last.then_inc(ln2_moments, 1)

            def x1_stats(g, b, k):
                dve.wait_ge(x1_ready, 4 * g + k + 1)
                nc.vector.bn_stats(stats2[:, k, :], x1[b][:, k, :]).then_inc(ln2_stats_done, 1)

            def step(g, b, has_pre=True, has_a=True, has_b=True, has_c=True, first=False):
                if has_a:
                    dve.wait_ge(hT_hi_ready, g + 1)
                    lo_part(hT_lo[:, :], turn[0][:, :], hT_hi[:, :], hT_lo_ready)
                if has_b:
                    x1_moments(g - 1, 1 - b)
                    nc.vector.tensor_copy(m_cur[1 - b][:, :], mask_cols[:, bass.ds(C * (g - 1), C)])
                if first:
                    dve.wait_ge(pick_steps, 2)
                    dve.wait_ge(sparse_loaded, 16 * SPARSE)
                    nc.vector.tensor_scalar(pick[:, :], pick[:, :], edge_col[:, 0:1], None,
                                            ALU.mult).then_inc(pick_steps, 1)
                    dve.wait_ge(w0_loaded, 16 * len(SLOT_RUNS))
                    nc.vector.tensor_copy(w0_hi[:, :],
                                          w0_full[:, :, :].rearrange("p r o -> p (r o)")).then_inc(w0_hi_ready, 1)
                if has_pre:
                    pre(g + 1, 1 - b)
                if has_b and shared(has_a, has_c):
                    half_norm2(g - 1, 1 - b, 0 if has_a else 1)
                late_c = has_c and (has_a or not has_b)
                if has_c and not late_c:
                    for n in range(4):
                        scale_step(g - 2, b, n)
                    finish(g - 2, b)
                if first:
                    dve.wait_ge(small_loaded, 16 * SMALL)
                    nc.vector.tensor_copy(b1_wide[:, :], b1_col[:, 0:1].to_broadcast([P, P])).then_inc(b1_ready, 1)
                if has_a:
                    split_adjT(g, b, 0)
                    split_adjT(g, b, 1)
                if has_b and not has_c:
                    split_w1()
                if has_a:
                    split_adjT(g, b, 2)
                    split_adjT(g, b, 3)
                if has_c and has_a:
                    scale_step(g - 2, b, 0)
                if has_a:
                    split_sums(g, b)
                if has_b:
                    dve.wait_ge(h2T_ready, g)
                    dve.wait_ge(h2T_hi_ready, g)
                    lo_part(h2T_lo[:, :], h2T[:, :], h2T_hi[:, :], h2T_lo_ready)
                if has_c and not has_b:
                    scale_step(g - 2, b, 0)
                if late_c:
                    scale_step(g - 2, b, 1)
                if has_a:
                    dve.wait_ge(atH_hi_ready, g + 1)
                    lo_part(atH_lo[:, :], agg_t[:, :], atH_hi[:, :], atH_lo_ready)
                if late_c:
                    scale_step(g - 2, b, 2)
                    scale_step(g - 2, b, 3)
                    finish(g - 2, b)
                if first:
                    split_c()
                if has_a:
                    dve.wait_ge(aH_hi_ready, g + 1)
                    lo_part(aH_lo[:, :], agg_a[:, :], aH_hi[:, :], aH_lo_ready)
                if has_b:
                    if not has_a:
                        attention_term(g - 1)
                    raw_values(g - 1)
                    if has_a:
                        attention_term(g - 1)
                if has_b and not has_a:
                    last_attention(g - 1, 1 - b)
                if first:
                    take_w1()
                    round_w1()
                if has_a:
                    dve.wait_ge(xb_ready, g + 1)
                    for k in range(C):
                        x1_max(g, b, k)

            def split_c():
                dve.wait_ge(c_hi_ready, 1)
                lo_part(c_rows[32:64, :], prod[0][32:64, 0:RO], c_rows[32:64, :], c_ready)

            def half_norm2(g, i, n):
                dve.wait_ge(ln2_ready, g + 1)
                if n > 0:
                    dve.wait_ge(h2T_done, g)
                half_norm(ln2, x1[i], h2, h2_steps, n + 1, h2_half_ready)

            def half_norm(t, src, dst, steps, n, ready):
                for k in (2, 3):
                    last = nc.vector.tensor_scalar(dst[:, k, :], src[:, k, :], t["scale"][:, k:k + 1],
                                                   t["shift"][:, k:k + 1], ALU.mult, ALU.add)
                last.then_inc(steps, 1)
                dve.wait_ge(steps, n)
                nc.vector.tensor_scalar(dst[:, 2:4, :], dst[:, 2:4, :], 0.0, None, ALU.max).then_inc(ready, 1)

            def take_w1():
                dve.wait_ge(w1_done, 1)
                nc.vector.tensor_copy(w1_full[:, 0:F], turn[1][:, P:2 * P])
                nc.vector.tensor_copy(mask_cols[:, :], turn[1][:, 2 * P:2 * P + G * C])
                nc.vector.tensor_copy(w1_full[:, F:F + 1], turn[1][:, 3 * P + 1:3 * P + 2])
                nc.vector.tensor_copy(wa1_full[:, :], turn[1][:, 3 * P:3 * P + 1].to_broadcast([P, P]))
                nc.vector.tensor_copy(b1_rows[:, :], turn[1][:, 0:P])
                nc.vector.reduce_sum(kappa[:, :], turn[1][:, 3 * P + 2:3 * P + 5], AX.X).then_inc(w1_taken, 1)

            def round_w1():
                dve.wait_ge(w1_taken, 1)
                nc.vector.tensor_copy(wa1_hi[:, :], wa1_full[:, :]).then_inc(wa1_hi_ready, 1)

            def split_w1():
                dve.wait_ge(wa1_hi_ready, 1)
                lo_part(wa1_lo[:, :], wa1_full[:, :], wa1_hi[:, :], w1_ready)

            nc.vector.memset(ones[:, :], 1.0).then_inc(ones_ready, 1)
            nc.vector.memset(raw[:, :, F:F + 1], 1.0).then_inc(out_free[0], 16)
            nc.vector.memset(sums_parts[:, :], 0.0).then_inc(out_free[1], 16)
            nc.vector.memset(pick[:, :], 0.0).then_inc(pick_steps, 1)
            dve.wait_ge(pick_steps, 1)
            nc.vector.memset(sums_parts[:, 16:17], 1.0)
            nc.vector.memset(sums_parts[:, 48:49], 1.0)
            for q, shift in ((0, 0), (32, C)):
                for c in (0, 8, 32):
                    nc.vector.memset(pick[q:q + 32, shift + c:shift + c + C], 1.0)
            for c in (16, 48):
                last = nc.vector.memset(pick[64:P, c:c + 1], 1.0)
            last.then_inc(pick_steps, 1)
            dve.wait_ge(ident_ready, 1)
            nc.vector.reduce_sum(chunk_rows[:, :], ident[:, 0:4 * C].rearrange("p (a k) -> p k a", k=C), AX.X)
            nc.vector.reduce_sum(chunk_rows_lo[:, :], ident[:, 32:32 + 2 * C].rearrange("p (a k) -> p k a", k=C),
                                 AX.X).then_inc(row_steps, 1)
            dve.wait_ge(row_steps, 1)
            nc.vector.tensor_tensor(chunk_rows[:, :], chunk_rows[:, :], chunk_rows_lo[:, :],
                                    ALU.add).then_inc(row_steps, 1)
            for n, c in ((2, 16), (3, 48)):
                dve.wait_ge(row_steps, n)
                last = nc.vector.tensor_tensor(chunk_rows[:, :], chunk_rows[:, :],
                                               ident[:, c:c + 1].to_broadcast([P, C]), ALU.add)
                last.then_inc(row_steps if n == 2 else rows_ready, 1)
            pre(0, 0)
            dve.wait_ge(ln1_ready, 1)
            half_norm(ln1, x_sb[0], h, h_steps, 1, h_half_ready)
            for k in range(C):
                dve.wait_ge(adj_hi_ready, k + 1)
                lo_part(adj_lo[0][:, k, :], adj_sb[0][:, k, :], adj_hi[0][:, k, :], adj_lo_ready)
            run(dve, step)

        @block.tensor
        def _(pe):
            def mm(dst, lhsT, rhs, start, stop):
                return nc.tensor.matmul(dst, lhsT, rhs, start=start, stop=stop)

            def turn_rows(dst, src, done):
                for k in range(C):
                    last = nc.tensor.transpose(dst[:, k * P:(k + 1) * P], src[:, k, :], ident[:, :])
                last.then_inc(done, 1)

            def turn_adj(b, m):
                for c in range(C):
                    last = nc.tensor.transpose(turn[1 - m % 2][:, c * P:(c + 1) * P],
                                               adj_sb[b][:, c, m * P:(m + 1) * P], ident[:, :])
                last.then_inc(adjT_done, 1)

            def aggregate(dst, hi, lo, k):
                mm(dst[:, :], h_hi[:, k, :], hi[:, k, :], k == 0, False)
                mm(dst[:, :], h_hi[:, k, :], lo[:, k, :], False, False)
                return mm(dst[:, :], h_lo[:, k, :], hi[:, k, :], False, k == C - 1)

            def times_w0(k, part, last_of_bank):
                hi, lo, c0, c1 = part
                nodes = slice(k * P, (k + 1) * P)
                dst = prod[k % 2][:, c0:c1]
                mm(dst, hi[:, nodes], w0_hi[:, c0:c1], False, False)
                mm(dst, hi[:, nodes], w0_lo[:, c0:c1], False, False)
                return mm(dst, lo[:, nodes], w0_hi[:, c0:c1], False, last_of_bank)

            H_PART = (hT_hi, hT_lo, 4 * F, 7 * F)
            ATH_PART = (atH_hi, atH_lo, 2 * F, 4 * F)
            AH_PART = (aH_hi, aH_lo, 0, 2 * F)

            def relations(g, k, has_c):
                mm(prod[k % 2][:, 0:BANK], sumsT[:, k, :], c_rows[:, 0:BANK], True, False)
                times_w0(k, ATH_PART, False)
                if k == 0 and has_c:
                    pe.wait_ge(out_ready, 2 * g - 2)
                mm(prod[k % 2][:, BANK:RO], sumsT[:, k, :], c_rows[:, BANK:RO], True, False)
                times_w0(k, H_PART, True)
                if k == 0:
                    pe.wait_ge(aH_lo_ready, g + 1)
                times_w0(k, AH_PART, True).then_inc(prod_done, 1)

            def attend(i):
                for j in range(C):
                    last = mm(prod[0][:, 256 * i:256 * i + WIDE], att[:, j, i * P:(i + 1) * P],
                              values[:, j, :], j == 0, j == C - 1)
                last.then_inc(att_done, 1)

            def attend_last(g):
                pe.wait_ge(values_ready, g + 1)
                pe.wait_ge(out_ready, 2 * g)
                for j in range(C):
                    pe.wait_ge(att_ready, 4 * g + j + 1)
                    for i in range(C):
                        last = mm(prod[i // 2][:, BANK * (i % 2):BANK * (i % 2) + WIDE],
                                  att[:, j, i * P:(i + 1) * P], values[:, j, :], j == 0, j == C - 1)
                        if j == C - 1:
                            last.then_inc(att_done, 1)

            def turn_sums(g):
                pe.wait_ge(sums_ready, g + 1)
                pe.wait_ge(adjT_ready, 4 * g + 4)
                nc.tensor.transpose(turn[0][:, 0:P], sums_parts[:, :], ident[:, :]).then_inc(sumsT_done, 1)

            def turn_w1():
                pe.wait_ge(b1_ready, 1)
                pe.wait_ge(small_loaded, 16 * SMALL)
                pe.wait_ge(adjT_ready, 3)
                nc.tensor.transpose(turn[1][:, P:2 * P], w1_nat[:, :], ident[:, :])
                nc.tensor.transpose(turn[1][:, 2 * P:2 * P + G * C], mask_rows[:, :], ident[0:G * C, 0:G * C])
                mm(turn[1][:, 3 * P:3 * P + 2], w1_nat[:, :], a_cols[:, :], True, True)
                nc.tensor.transpose(turn[1][:, 0:P], b1_wide[:, :], ident[:, :])
                mm(turn[1][:, 3 * P + 2:3 * P + 4], b1_wide[:, :], a_cols[:, :], True, True)
                mm(turn[1][:, 3 * P + 4:3 * P + 5], ones[:, :], att_b_col[:, :], True, True).then_inc(w1_done, 1)

            def step(g, b, has_pre=True, has_a=True, has_b=True, has_c=True, first=False):
                if has_a:
                    pe.wait_ge(h_ready, g + 1)
                    if first:
                        pe.wait_ge(h_half_ready, 1)
                    wait(pe, sumsT_ready, 4 * g)
                    turn_rows(turn[0], h, hT_done)
                    if first:
                        pe.wait_ge(adj_loaded[0], 16)
                        turn_adj(b, 0)
                    pe.wait_ge(h_lo_ready, g + 1)
                    pe.wait_ge(adj_lo_ready, 4 * g + 2)
                    wait(pe, sig_ready, 4 * g - 4)
                    aggregate(agg_t, adj_hi[b], adj_lo[b], 0)
                    aggregate(agg_t, adj_hi[b], adj_lo[b], 1)
                    if not first:
                        wait(pe, h2T_hi_ready, g - 1)
                        turn_adj(b, 0)
                    pe.wait_ge(adj_lo_ready, 4 * g + 4)
                    aggregate(agg_t, adj_hi[b], adj_lo[b], 2)
                    pe.wait_ge(hT_lo_ready, g + 1)
                    turn_adj(b, 1)
                    aggregate(agg_t, adj_hi[b], adj_lo[b], 3).then_inc(atH_done, 1)
                    pe.wait_ge(adjT_ready, 4 * g + 1)
                    turn_adj(b, 2)
                if first:
                    pe.wait_ge(pick_steps, 3)
                    pe.wait_ge(sparse_loaded, 16 * SPARSE)
                    mm(prod[0][:, 0:BANK], pick[:, :], wrel[:, 0:BANK], True, True)
                    mm(prod[0][:, BANK:RO], pick[:, :], wrel[:, BANK:RO], True, True).then_inc(c_done, 1)
                if has_c and not has_b:
                    attend_last(g - 2)
                elif has_c:
                    pe.wait_ge(values_ready, g - 1)
                    pe.wait_ge(att_ready, 4 * g - 4)
                    pe.wait_ge(max_done, 4 * g - 1)
                    attend(0)
                if has_a:
                    pe.wait_ge(adjT_ready, 4 * g + 2)
                    turn_adj(b, 3)
                if has_c and has_b:
                    for i in range(1, C - 1 if has_a else C):
                        attend(i)
                if has_b:
                    pe.wait_ge(h2_ready, g)
                    if shared(has_a, has_c):
                        pe.wait_ge(h2_half_ready, 1 if has_a else 2)
                    if has_a:
                        pe.wait_ge(adjT_ready, 4 * g + 3)
                    turn_rows(turn[1], h2, h2T_done)
                if has_c and has_b and has_a:
                    attend(C - 1)
                if has_a:
                    wait(pe, aH_lo_ready, g)
                    for k in range(C):
                        if first and k == 2:
                            turn_w1()
                        pe.wait_ge(adjT_lo_ready, 4 * g + k + 1)
                        last = aggregate(agg_a, adjT_hi, adjT_lo, k)
                    last.then_inc(aH_done, 1)
                if has_b:
                    if not has_c:
                        pe.wait_ge(w1_ready, 1)
                    pe.wait_ge(h2T_ready, g)
                    pe.wait_ge(max_done, 4 * g)
                    for j in range(C):
                        dst = prod[1][:, 256 * j:256 * j + WIDE]
                        nodes = slice(j * P, (j + 1) * P)
                        if j == 2 and has_a:
                            turn_sums(g)
                        last = mm(dst, h2T[:, nodes], w1_full[:, :], True, True)
                    last.then_inc(hw_done, 1)
                if has_a and not has_b:
                    turn_sums(g)
                if has_b:
                    pe.wait_ge(h2T_lo_ready, g)
                    if has_a:
                        pe.wait_ge(atH_lo_ready, g + 1)
                    mm(agg_t[:, :], wa1_hi[:, :], h2T_hi[:, :], True, False)
                    mm(agg_t[:, :], wa1_hi[:, :], h2T_lo[:, :], False, False)
                    mm(agg_t[:, :], wa1_lo[:, :], h2T_hi[:, :], False, True).then_inc(s1_done, 1)
                if has_a:
                    for k in range(C):
                        pe.wait_ge(sumsT_ready, 4 * g + k + 1)
                        if k == 0 and has_c:
                            pe.wait_ge(out_ready, 2 * g - 3)
                        elif k == 1 and has_b:
                            pe.wait_ge(s2_ready, g)
                            pe.wait_ge(raw_ready, g)
                        elif k >= 2:
                            pe.wait_ge(max_done, 4 * g + k - 1)
                        if first and k == 0:
                            pe.wait_ge(w0_ready, 1)
                            pe.wait_ge(c_ready, 1)
                        relations(g, k, has_c)
                if first:
                    pe.wait_ge(w1_taken, 1)

            pe.wait_ge(ident_ready, 1)
            run(pe, step)


_INS = ['x', 'adj', 'nodemask', 'L0_gnn_W', 'L0_gnn_W_edges', 'L0_gnn_b', 'L1_gnn_W', 'L1_gnn_b', 'L1_gnn_a1',
        'L1_gnn_a2', 'L1_gnn_att_b']


def kernel(**inputs):
    import numpy as _np
    import concourse.bacc as _bacc
    from concourse import mybir as _mybir
    from concourse.bass_utils import run_bass_kernel_spmd as _run

    nc = _bacc.Bacc("TRN2", target_bir_lowering=False, num_devices=1)
    arrays, args = {}, []
    for name in _INS:
        a = _np.ascontiguousarray(inputs[name])
        if name == 'L1_gnn_att_b':
            a = a.reshape(1, 1)
        arrays[f"in_{name}_dram"] = a
        args.append(nc.dram_tensor(f"in_{name}_dram", a.shape, _mybir.dt.from_np(a.dtype), kind="ExternalInput").ap())
    shape = inputs['x'].shape
    args.append(nc.dram_tensor("out_0_dram", shape, _mybir.dt.float32, kind="ExternalOutput").ap())
    build(nc, *args)
    r = _run(nc, [arrays], core_ids=[0])
    return r.results[0]["out_0_dram"]
```
